# Optimizing a Trainium2 kernel written in Bass

```python
import numpy as np
import jax
import jax.numpy as jnp

def _softmax(x, axis=-1):
    return jax.nn.softmax(x, axis=axis)

def _gelu(x):
    return jax.nn.gelu(x, approximate=True)

def _silu(x):
    return jax.nn.silu(x)

def _sigmoid(x):
    return jax.nn.sigmoid(x)

def _layernorm(x, axis=-1, eps=1e-05):
    m = jnp.mean(x, axis=axis, keepdims=True)
    v = jnp.var(x, axis=axis, keepdims=True)
    return (x - m) / jnp.sqrt(v + eps)

def _scatter_add(tgt, idx, src, axis=0):
    return tgt.at[idx].add(src)

def _segment_sum(src, seg, n):
    return jax.ops.segment_sum(src, seg, n)
kernel_name = 'mk_cond_resid_d4_seqx_r8_5e7a43'

def setup_inputs(seed: int=0):
    np.random.seed(seed)
    _w = jnp.asarray

    def _rec_inputs():
        import jax
        import jax.numpy as jnp
        _rk = jax.random.key(seed)
        x = -0.0005207 + 1.001 * jax.random.normal(jax.random.fold_in(_rk, 1), (64, 32, 512), jnp.float32)
        _lenS = 32 - jax.random.randint(jax.random.fold_in(_rk, 7), (64,), 0, max(1, 32 // 4) + 1, jnp.int32)
        _lenS2 = 32 - jax.random.randint(jax.random.fold_in(_rk, 8), (64,), 0, max(1, 32 // 4) + 1, jnp.int32)
        itok_Bx16_0_63 = jax.random.randint(jax.random.fold_in(_rk, 11), (64, 16), 0, 64, jnp.int32)
        itok_B_207_1644 = jax.random.randint(jax.random.fold_in(_rk, 12), (64,), 207, 1645, jnp.int32)
        itok_B_6_15 = jax.random.randint(jax.random.fold_in(_rk, 13), (64,), 6, 16, jnp.int32)
        itok_B_3_7 = jax.random.randint(jax.random.fold_in(_rk, 14), (64,), 3, 8, jnp.int32)
        itok_B_0_23 = jax.random.randint(jax.random.fold_in(_rk, 15), (64,), 0, 24, jnp.int32)
        return (x, itok_Bx16_0_63, itok_B_207_1644, itok_B_6_15, itok_B_3_7, itok_B_0_23)
    x, itok_Bx16_0_63, itok_B_207_1644, itok_B_6_15, itok_B_3_7, itok_B_0_23 = _rec_inputs()

    def _L0_cond_setup():
        import jax, jax.numpy as jnp
        import numpy as np
        B, S, HID = (4, 128, 512)
        D, HQ, HK = (128, 32, 8)
        PAGES, PSIZE, NPP = (64, 32, 16)
        THETA = 10000.0
        EPS = 1e-06
        SCALE = 1.0 / float(np.sqrt(D))

        def _rmsnorm(t, w):
            var = jnp.mean(t * t, axis=-1, keepdims=True)
            return t * jax.lax.rsqrt(var + EPS) * w

        def _rope(t, pos):
            inv_freq = 1.0 / THETA ** (jnp.arange(0, D, 2, dtype=jnp.float32) / D)
            freqs = pos[..., None].astype(jnp.float32) * inv_freq
            cos = jnp.cos(freqs)[:, :, None, :]
            sin = jnp.sin(freqs)[:, :, None, :]
            t1, t2 = (t[..., :D // 2], t[..., D // 2:])
            return jnp.concatenate([t1 * cos - t2 * sin, t2 * cos + t1 * sin], axis=-1)
        key = jax.random.key(seed)
        ks = jax.random.split(key, 10)
        x = jax.random.normal(ks[0], (B, S, HID), jnp.float32)
        Wq = jax.random.normal(ks[1], (HQ * D, HID), jnp.float32) * 0.02
        Wk = jax.random.normal(ks[2], (HK * D, HID), jnp.float32) * 0.02
        Wv = jax.random.normal(ks[3], (HK * D, HID), jnp.float32) * 0.02
        Wo = jax.random.normal(ks[4], (HID, HQ * D), jnp.float32) * 0.02
        q_norm_w = jax.random.uniform(ks[5], (D,), jnp.float32)
        k_norm_w = jax.random.uniform(ks[6], (D,), jnp.float32)
        k_cache = jax.random.normal(ks[7], (PAGES, PSIZE, HK, D), jnp.float32)
        v_cache = jax.random.normal(ks[8], (PAGES, PSIZE, HK, D), jnp.float32)
        block_table = jnp.arange(B * NPP, dtype=jnp.int32).reshape(B, NPP)
        cache_seqlens = jax.random.randint(ks[9], (B,), 0, 475).astype(jnp.int32)
        return dict(x=x, Wq=Wq, Wk=Wk, Wv=Wv, Wo=Wo, q_norm_w=q_norm_w, k_norm_w=k_norm_w, k_cache=k_cache, v_cache=v_cache, block_table=block_table, cache_seqlens=cache_seqlens)
    _L0_cond_all = _L0_cond_setup()
    _L0_cond_in = {k: v for k, v in _L0_cond_all.items() if k in ('Wq', 'Wk', 'Wv', 'Wo', 'q_norm_w', 'k_norm_w', 'k_cache', 'v_cache')}
    del _L0_cond_all

    def _L1_cond_setup():
        import jax, jax.numpy as jnp
        import numpy as np
        B, S, D_IN, D_OUT = (4, 256, 512, 512)
        RANK, MAX_LORAS = (16, 32)
        key = jax.random.key(seed)
        ks = jax.random.split(key, 6)
        x = jax.random.normal(ks[0], (B, S, D_IN), dtype=jnp.float32)
        adapter_ids = jax.random.randint(ks[1], (B,), 0, MAX_LORAS)
        base_weight = jax.random.normal(ks[2], (D_OUT, D_IN), dtype=jnp.float32) * D_IN ** (-0.5)
        base_bias = jax.random.normal(ks[3], (D_OUT,), dtype=jnp.float32) * 0.01
        lora_A_w = jax.random.normal(ks[4], (MAX_LORAS, RANK, D_IN), dtype=jnp.float32) * D_IN ** (-0.5)
        lora_B_w = jax.random.normal(ks[5], (MAX_LORAS, D_OUT, RANK), dtype=jnp.float32) * RANK ** (-0.5)
        return {'x': x, 'adapter_ids': adapter_ids, 'base_weight': base_weight, 'base_bias': base_bias, 'lora_A_w': lora_A_w, 'lora_B_w': lora_B_w}
    _L1_cond_all = _L1_cond_setup()
    _L1_cond_in = {k: v for k, v in _L1_cond_all.items() if k in ('base_weight', 'base_bias', 'lora_A_w', 'lora_B_w')}
    del _L1_cond_all

    def _L2_cond_setup():
        import jax, jax.numpy as jnp
        import numpy as np
        RANK = 16
        ALPHA = 16.0
        SCALING = ALPHA / RANK
        N_ADAPTERS = 8
        IN_F = 512
        OUT_F = 512
        BATCH = 4
        SEQ = 256
        key = jax.random.key(seed)
        kx, ka, kb, ki = jax.random.split(key, 4)
        x = jax.random.normal(kx, (BATCH, SEQ, IN_F), dtype=jnp.float32)
        A = jax.random.normal(ka, (N_ADAPTERS, OUT_F, RANK), dtype=jnp.float32) * 0.02
        B = jax.random.normal(kb, (N_ADAPTERS, RANK, IN_F), dtype=jnp.float32) * 0.02
        adapter_ids = jax.random.randint(ki, (BATCH,), 0, N_ADAPTERS, dtype=jnp.int32)
        return {'x': x, 'A': A, 'B': B, 'adapter_ids': adapter_ids}
    _L2_cond_all = _L2_cond_setup()
    _L2_cond_in = {k: v for k, v in _L2_cond_all.items() if k in ('A', 'B')}
    del _L2_cond_all

    def _L3_cond_setup():
        import jax, jax.numpy as jnp
        import numpy as np
        R = 16
        ALPHA = 32
        SCALING = ALPHA / R
        SLOTS = 32
        IN_F = 512
        OUT_F = 512
        B, T = (8, 128)
        key = jax.random.key(seed)
        k1, k2, k3, k4, k5, k6 = jax.random.split(key, 6)
        x = jax.random.normal(k1, (B, T, IN_F), dtype=jnp.float32)
        adapter_mapping = jax.random.randint(k2, (B,), 0, SLOTS, dtype=jnp.int32)
        W = jax.random.normal(k3, (OUT_F, IN_F), dtype=jnp.float32) * 0.02
        b = jax.random.normal(k4, (OUT_F,), dtype=jnp.float32) * 0.02
        lora_As = jax.random.normal(k5, (SLOTS, IN_F, R), dtype=jnp.float32) * 0.02
        lora_Bs = jax.random.normal(k6, (SLOTS, R, OUT_F), dtype=jnp.float32) * 0.02
        return {'x': x, 'adapter_mapping': adapter_mapping, 'W': W, 'b': b, 'lora_As': lora_As, 'lora_Bs': lora_Bs}
    _L3_cond_all = _L3_cond_setup()
    _L3_cond_in = {k: v for k, v in _L3_cond_all.items() if k in ('W', 'b', 'lora_As', 'lora_Bs')}
    del _L3_cond_all
    return {'x': x, 'itok_Bx16_0_63': itok_Bx16_0_63, 'itok_B_207_1644': itok_B_207_1644, 'itok_B_6_15': itok_B_6_15, 'itok_B_3_7': itok_B_3_7, 'itok_B_0_23': itok_B_0_23, 'L0_cond_Wq': _L0_cond_in['Wq'], 'L0_cond_Wk': _L0_cond_in['Wk'], 'L0_cond_Wv': _L0_cond_in['Wv'], 'L0_cond_Wo': _L0_cond_in['Wo'], 'L0_cond_q_norm_w': _L0_cond_in['q_norm_w'], 'L0_cond_k_norm_w': _L0_cond_in['k_norm_w'], 'L0_cond_k_cache': _L0_cond_in['k_cache'], 'L0_cond_v_cache': _L0_cond_in['v_cache'], 'L1_cond_base_weight': _L1_cond_in['base_weight'], 'L1_cond_base_bias': _L1_cond_in['base_bias'], 'L1_cond_lora_A_w': _L1_cond_in['lora_A_w'], 'L1_cond_lora_B_w': _L1_cond_in['lora_B_w'], 'L2_cond_A': _L2_cond_in['A'], 'L2_cond_B': _L2_cond_in['B'], 'L3_cond_W': _L3_cond_in['W'], 'L3_cond_b': _L3_cond_in['b'], 'L3_cond_lora_As': _L3_cond_in['lora_As'], 'L3_cond_lora_Bs': _L3_cond_in['lora_Bs']}

def reference(x, itok_Bx16_0_63, itok_B_207_1644, itok_B_6_15, itok_B_3_7, itok_B_0_23, L0_cond_Wq, L0_cond_Wk, L0_cond_Wv, L0_cond_Wo, L0_cond_q_norm_w, L0_cond_k_norm_w, L0_cond_k_cache, L0_cond_v_cache, L1_cond_base_weight, L1_cond_base_bias, L1_cond_lora_A_w, L1_cond_lora_B_w, L2_cond_A, L2_cond_B, L3_cond_W, L3_cond_b, L3_cond_lora_As, L3_cond_lora_Bs):
    import jax
    import jax.numpy as jnp

    def _L0_cond_ref(x, Wq, Wk, Wv, Wo, q_norm_w, k_norm_w, k_cache, v_cache, block_table, cache_seqlens):
        import jax, jax.numpy as jnp
        import numpy as np
        B, S, HID = (4, 128, 512)
        D, HQ, HK = (128, 32, 8)
        PAGES, PSIZE, NPP = (64, 32, 16)
        THETA = 10000.0
        EPS = 1e-06
        SCALE = 1.0 / float(np.sqrt(D))

        def _rmsnorm(t, w):
            var = jnp.mean(t * t, axis=-1, keepdims=True)
            return t * jax.lax.rsqrt(var + EPS) * w

        def _rope(t, pos):
            inv_freq = 1.0 / THETA ** (jnp.arange(0, D, 2, dtype=jnp.float32) / D)
            freqs = pos[..., None].astype(jnp.float32) * inv_freq
            cos = jnp.cos(freqs)[:, :, None, :]
            sin = jnp.sin(freqs)[:, :, None, :]
            t1, t2 = (t[..., :D // 2], t[..., D // 2:])
            return jnp.concatenate([t1 * cos - t2 * sin, t2 * cos + t1 * sin], axis=-1)
        bsz, seqlen, _ = x.shape
        q = jnp.einsum('bsd,ed->bse', x, Wq).reshape(bsz, seqlen, HQ, D)
        k = jnp.einsum('bsd,ed->bse', x, Wk).reshape(bsz, seqlen, HK, D)
        v = jnp.einsum('bsd,ed->bse', x, Wv).reshape(bsz, seqlen, HK, D)
        q = _rmsnorm(q, q_norm_w)
        k = _rmsnorm(k, k_norm_w)
        pos = cache_seqlens[:, None] + jnp.arange(seqlen)[None, :]
        q = _rope(q, pos)
        k = _rope(k, pos)
        L = NPP * PSIZE
        kc = k_cache[block_table].reshape(bsz, L, HK, D)
        vc = v_cache[block_table].reshape(bsz, L, HK, D)
        k_all = jnp.concatenate([kc, k], axis=1)
        v_all = jnp.concatenate([vc, v], axis=1)
        valid_c = jnp.arange(L)[None, :] < cache_seqlens[:, None]
        valid = jnp.concatenate([valid_c, jnp.ones((bsz, seqlen), dtype=bool)], axis=1)
        rep = HQ // HK
        k_all = jnp.repeat(k_all, rep, axis=2)
        v_all = jnp.repeat(v_all, rep, axis=2)
        scores = jnp.einsum('bqhd,bkhd->bhqk', q, k_all) * SCALE
        scores = jnp.where(valid[:, None, None, :], scores, -1e+30)
        probs = jax.nn.softmax(scores, axis=-1)
        o = jnp.einsum('bhqk,bkhd->bqhd', probs, v_all)
        o = o.reshape(bsz, seqlen, HQ * D)
        return jnp.einsum('bse,de->bsd', o, Wo)

    def _L1_cond_ref(x, adapter_ids, base_weight, base_bias, lora_A_w, lora_B_w):
        import jax, jax.numpy as jnp
        import numpy as np
        B, S, D_IN, D_OUT = (4, 256, 512, 512)
        RANK, MAX_LORAS = (16, 32)
        result = jnp.einsum('bsd,od->bso', x, base_weight) + base_bias
        A = lora_A_w[adapter_ids]
        Bw = lora_B_w[adapter_ids]
        h = jnp.einsum('bsd,brd->bsr', x, A)
        lora_out = jnp.einsum('bsr,bor->bso', h, Bw)
        result = result + lora_out
        return result.astype(x.dtype)

    def _L2_cond_ref(x, A, B, adapter_ids):
        import jax, jax.numpy as jnp
        import numpy as np
        RANK = 16
        ALPHA = 16.0
        SCALING = ALPHA / RANK
        N_ADAPTERS = 8
        IN_F = 512
        OUT_F = 512
        BATCH = 4
        SEQ = 256
        B_sel = B[adapter_ids]
        A_sel = A[adapter_ids]
        Bx = jnp.einsum('bni,bri->bnr', x, B_sel)
        out = jnp.einsum('bnr,bor->bno', Bx, A_sel)
        return out * SCALING

    def _L3_cond_ref(x, adapter_mapping, W, b, lora_As, lora_Bs):
        import jax, jax.numpy as jnp
        import numpy as np
        R = 16
        ALPHA = 32
        SCALING = ALPHA / R
        SLOTS = 32
        IN_F = 512
        OUT_F = 512
        B, T = (8, 128)
        base_out = jnp.einsum('bti,oi->bto', x, W) + b
        A = lora_As[adapter_mapping]
        Bm = lora_Bs[adapter_mapping]
        lora_h = jnp.einsum('bti,bir->btr', x, A)
        lora_out = jnp.einsum('btr,bro->bto', lora_h, Bm)
        return base_out + lora_out * SCALING
    x = x + _L0_cond_ref(x, L0_cond_Wq, L0_cond_Wk, L0_cond_Wv, L0_cond_Wo, L0_cond_q_norm_w, L0_cond_k_norm_w, L0_cond_k_cache, L0_cond_v_cache, itok_Bx16_0_63, itok_B_207_1644)
    x = x + _L1_cond_ref(x, itok_B_6_15, L1_cond_base_weight, L1_cond_base_bias, L1_cond_lora_A_w, L1_cond_lora_B_w)
    x = x + _L2_cond_ref(x, L2_cond_A, L2_cond_B, itok_B_3_7)
    x = x + _L3_cond_ref(x, itok_B_0_23, L3_cond_W, L3_cond_b, L3_cond_lora_As, L3_cond_lora_Bs)
    return x

_drawn_inputs = setup_inputs


def setup_inputs(seed=0):
    import zlib

    import numpy as np

    out = dict(_drawn_inputs(seed))
    spreads = {}
    factors = {'L0_cond_Wk': 8.0,
     'L0_cond_Wv': 8.0,
     'L0_cond_k_norm_w': 8.0,
     'L1_cond_base_bias': 24.441,
     'L3_cond_b': 6.421,
     'L0_cond_k_cache': 4.304,
     'L0_cond_v_cache': 3.092}
    for name, (base, spread) in spreads.items():
        noise = np.random.default_rng([zlib.crc32(name.encode()), seed]).standard_normal(out[name].shape)
        drawn = base * np.exp(spread * noise) if base else spread * noise
        out[name] = jnp.asarray(drawn.astype(out[name].dtype))
    for name, factor in factors.items():
        out[name] = (out[name] * factor).astype(out[name].dtype)
    return out
```

```python
from contextlib import ExitStack

import numpy as np

import concourse.bass as bass
from concourse import mybir

F32 = mybir.dt.float32
F32R = mybir.dt.float32r
I32 = mybir.dt.int32
ALU = mybir.AluOpType
ACT = mybir.ActivationFunctionType

P = 128
BATCH, SEQ, HID = 64, 32, 512
D, HQ, HK = 128, 32, 8
REP = HQ // HK
PAGES, PSIZE, NPP = 64, 32, 16
CACHED = NPP * PSIZE
KEYS = CACHED + SEQ
TOKENS = BATCH * SEQ
TILES = TOKENS // P
BPT = P // SEQ
KT = HID // P
CH = 512
HPC = CH // D
V_CHUNKS = HK * D // CH
K_CHUNKS = HK * D // CH
Q_CHUNKS = HQ * D // CH
THETA, EPS = 10000.0, 1e-6
SCALE = 1.0 / float(np.sqrt(D))
MASKED = 1e30
RANK = 16
LORA_SCALE = 2.0
PI_BELOW = float(np.nextafter(np.float32(np.pi), np.float32(0)))
TWO_PI_1 = 6.28125
TWO_PI_2 = 0.0019340515136718750
TWO_PI_3 = float(np.float64(2 * np.pi) - TWO_PI_1 - TWO_PI_2)
TABLE_STEPS = 20


def wait(eng, sem, count):
    if isinstance(count, int) and count <= 0:
        return
    eng.wait_ge(sem, count)


def wait_all(eng, passed, *waits):
    for sem, count in waits:
        wait(eng, sem, count)
    eng.sem_inc(passed, 1)


def build_identity(eng, ident, ready):
    eng.memset(ident[:, :], 0.0).then_inc(ready, 1)
    eng.wait_ge(ready, 1)
    eng.affine_select(out=ident[:, :], in_=ident[:, :], compare_op=ALU.not_equal, fill=1.0,
                      base=0, pattern=[[-1, P]], channel_multiplier=1).then_inc(ready, 1)


def project(nc, ps, a, scratch):
    with ExitStack() as ctx:
        def sb(name, shape, dt=F32):
            return ctx.enter_context(nc.sbuf_tensor("p_" + name, shape, dt))

        def sem(name):
            return ctx.enter_context(nc.semaphore("p_" + name))

        xstage = sb("xstage", [P, KT, 512])
        xh = sb("xh", [P, 4, KT, 512], F32R)
        xl = sb("xl", [P, 4, KT, 512], F32R)
        wraw = sb("wraw", [P, 2, KT, CH])
        wh = sb("wh", [P, 2, KT, CH], F32R)
        wl = sb("wl", [P, 2, KT, CH], F32R)
        ident = sb("ident", [P, P])
        pos_i = sb("pos_i", [P, TILES], I32)
        pos = sb("pos", [P, TILES])
        row_in_seq = sb("row_in_seq", [P, 1])
        inv_freq = sb("inv_freq", [P, D // 2])
        norm_w = sb("norm_w", [P, 2, D])
        angle = sb("angle", [P, TILES, D // 2])
        turns = sb("turns", [P, TILES, D // 2], I32)
        sine = sb("sine", [P, TILES, D // 2])
        cosine = turns[:, :, :].bitcast(F32)
        cos_w = sb("cos_w", [P, 2, TILES, D])
        sin_w = sb("sin_w", [P, 2, TILES, D])
        proj = sb("proj", [P, 2, HPC, D])
        square = sb("square", [P, 2, HPC, D])
        ss = sb("ss", [P, 2, HPC])
        mean_sq = sb("mean_sq", [P, 2, HPC])
        minus_half = sb("minus_half", [P, HPC])
        rinv = sb("rinv", [P, 2, HPC])
        by_cos = sb("by_cos", [P, HPC, D])
        by_sin = sb("by_sin", [P, 2, HPC, D])
        rotated = sb("rotated", [P, HPC, D])
        normed = sb("normed", [P, 2, HPC, D])
        vout = sb("vout", [P, 2, CH])
        kout = sb("kout", [P, 2, BPT, HPC, SEQ])
        qout_h = sb("qout_h", [P, 2, BPT, HPC, SEQ], F32R)
        qout_l = sb("qout_l", [P, 2, BPT, HPC, SEQ], F32R)

        consts_loaded = sem("consts_loaded")
        x_loaded = sem("x_loaded")
        x_hi_ready = sem("x_hi_ready")
        x_lo_ready = sem("x_lo_ready")
        w_loaded = [sem("w_loaded0"), sem("w_loaded1")]
        w_hi_ready = sem("w_hi_ready")
        w_lo_ready = sem("w_lo_ready")
        ident_ready = sem("ident_ready")
        table_step = sem("table_step")
        sines_ready = sem("sines_ready")
        mm_done = sem("mm_done")
        v_copied = sem("v_copied")
        v_stored = [sem("v_stored0"), sem("v_stored1")]
        proj_ready = sem("proj_ready")
        ss_ready = sem("ss_ready")
        pool_step = sem("pool_step")
        by_sin_ready = sem("by_sin_ready")
        rinv_ready = sem("rinv_ready")
        by_cos_ready = sem("by_cos_ready")
        rotated_ready = sem("rotated_ready")
        normed_ready = sem("normed_ready")
        turned = sem("turned")
        turned_read = sem("turned_read")
        k_copied = sem("k_copied")
        q_hi_copied = sem("q_hi_copied")
        q_lo_copied = sem("q_lo_copied")
        stored = [sem("stored0"), sem("stored1")]

        PAIR = 2 * TILES
        V_UNITS = V_CHUNKS * TILES
        K_UNITS = K_CHUNKS * TILES
        PAIRS = (V_CHUNKS + K_CHUNKS + Q_CHUNKS) // 2
        N_ROT = (PAIRS - 1) * PAIR
        LAG = 2
        block = ctx.enter_context(nc.Block())

        def over_pairs(eng, body):
            for pair in range(3):
                body(pair, pair)
            with eng.Fori(3, PAIRS) as pair:
                body(pair, 3)

        def rot_kind(pair_kind, n):
            kind = pair_kind + (n // PAIR)
            return None if kind < 1 else "k" if kind == 1 else "q"

        @block.sync
        def _(sp):
            def load_w(chunk, par):
                wait(sp, w_lo_ready, KT * (chunk - 1))
                sp.dma_start(wraw[:, par, :, :], a["w_all"][chunk] if isinstance(chunk, int)
                             else a["w_all"][bass.ds(chunk, 1), :, :, :].rearrange("a p k n -> p (a k) n"))\
                  .then_inc(w_loaded[par], 16)

            load_w(0, 0)
            for quarter in range(4):
                wait(sp, x_lo_ready, quarter)
                sp.dma_start(xstage[:, :, :], a["xT"][:, quarter, :, :]).then_inc(x_loaded, 16)
                if quarter == 0:
                    load_w(1, 1)

            def store(pair, n, kind):
                r = PAIR * (pair - 1) + n
                par, t, c = n % 2, n % TILES, (n % PAIR) // TILES
                seqs = slice(BPT * t, BPT * t + BPT)
                if kind == "k":
                    wait(sp, k_copied, r + 1)
                    dst = scratch["k"][seqs, :, HPC * c:HPC * c + HPC, :]
                    sp.dma_start(dst.rearrange("b d h s -> d b (h s)"),
                                 kout[:, par, :, :, :].rearrange("d b h s -> d b (h s)")).then_inc(stored[par], 16)
                    return
                head = (2 * (pair - 2) + n // TILES) * HPC
                if not isinstance(head, int):
                    head = sp.snap(head)
                for name, src, done in (("qh", qout_h, q_hi_copied), ("ql", qout_l, q_lo_copied)):
                    wait(sp, done, r - K_UNITS + 1)
                    dst = scratch[name][seqs, :, bass.ds(head, HPC), :]
                    sp.dma_start(dst.rearrange("b d h s -> d b (h s)"),
                                 src[:, par, :, :, :].bitcast(F32).rearrange("d b h s -> d b (h s)"))\
                      .then_inc(stored[par], 16)

            def body(pair, kind):
                for n in range(PAIR):
                    t, c = n % TILES, n // TILES
                    if t == 0 and kind * 2 + c >= 1:
                        chunk = 2 * pair + c + 1
                        if not isinstance(pair, int):
                            chunk = sp.snap(chunk)
                        load_w(chunk, (c + 1) % 2)
                    if kind == 0:
                        wait(sp, v_copied, n + 1)
                        sp.dma_start(scratch["v"][P * t:P * t + P, CH * c:CH * c + CH], vout[:, n % 2, :])\
                          .then_inc(v_stored[n % 2], 16)
                    m = n - LAG
                    if rot_kind(kind, m):
                        store(pair, m, rot_kind(kind, m))

            over_pairs(sp, body)
            for m in range(-LAG, 0):
                store(PAIRS, m, "q")
            for par in range(2):
                sp.wait_ge(v_stored[par], 16 * V_UNITS // 2)
                sp.wait_ge(stored[par], 16 * K_UNITS // 2 + 32 * (N_ROT - K_UNITS) // 2)
            sp.wait_ge(w_loaded[0], 16 * (PAIRS + 1))

        @block.gpsimd
        def _(pool):
            pool.dma_start(pos_i[:, :], a["seqlen_by_tile"]).then_inc(consts_loaded, 16)
            pool.dma_start(row_in_seq[:, :], a["row_in_seq"]).then_inc(consts_loaded, 16)
            pool.dma_start(inv_freq[:, :], a["inv_freq"]).then_inc(consts_loaded, 16)
            pool.dma_start(norm_w[:, 0, :], a["k_norm"]).then_inc(consts_loaded, 16)
            pool.dma_start(norm_w[:, 1, :], a["q_norm"]).then_inc(consts_loaded, 16)
            build_identity(pool, ident, ident_ready)
            pool.memset(minus_half[:, :], -0.5).then_inc(pool_step, 1)

            def body(pair, kind):
                if kind == 0:
                    return
                side = 0 if kind == 1 else 1
                for n in range(PAIR):
                    r, par, t = PAIR * (pair - 1) + n, n % 2, n % TILES
                    wait(pool, proj_ready, r + 1)
                    wait(pool, rotated_ready, r - 1)
                    if kind == 1 and n == 0:
                        pool.wait_ge(table_step, TABLE_STEPS)
                    swapped = proj[:, par, :, :].rearrange("p h (a c) -> p h a c", a=2)[:, :, ::-1, :]
                    pool.tensor_tensor(by_sin[:, par, :, :].rearrange("p h (a c) -> p h a c", a=2), swapped,
                                       sin_w[:, side, t:t + 1, :].rearrange("p o (a c) -> p o a c", a=2)
                                       .to_broadcast([P, HPC, 2, D // 2]), ALU.mult).then_inc(by_sin_ready, 1)
                    pool.wait_ge(table_step, TABLE_STEPS)
                    pool.wait_ge(ss_ready, r + 1)
                    pool.tensor_scalar(mean_sq[:, par, :], ss[:, par, :], 1.0 / D, EPS, ALU.mult, ALU.add)\
                        .then_inc(pool_step, 1)
                    pool.wait_ge(pool_step, r + 2)
                    wait(pool, normed_ready, r - 1)
                    pool.tensor_tensor(rinv[:, par, :], mean_sq[:, par, :], minus_half[:, :], ALU.pow)\
                        .then_inc(rinv_ready, 1)

            over_pairs(pool, body)

        @block.scalar
        def _(act):
            def split_next(pair, n):
                t, c = n % TILES, n // TILES
                if t % 3 == 0 and 3 <= t <= 12:
                    kt, par = t // 3 - 1, (c + 1) % 2
                    act.wait_ge(w_loaded[par], 16 * (pair + 1 + c))
                    wait(act, mm_done, PAIR * pair + TILES * c)
                    act.copy(wh[:, par, kt, :], wraw[:, par, kt, :]).then_inc(w_hi_ready, 1)

            act.wait_ge(w_loaded[0], 16)
            for kt in range(KT):
                act.copy(wh[:, 0, kt, :], wraw[:, 0, kt, :]).then_inc(w_hi_ready, 1)
            for quarter in range(4):
                act.wait_ge(x_loaded, 16 * (quarter + 1))
                act.copy(xh[:, quarter, :, :], xstage[:, :, :]).then_inc(x_hi_ready, 1)
            act.wait_ge(table_step, 9)
            act.activation(sine[:, :, :], angle[:, :, :], ACT.Sin).then_inc(sines_ready, 1)
            act.activation(cosine, angle[:, :, :], ACT.Sin, scale=0.5).then_inc(sines_ready, 1)

            def turned_out(pair, n, kind):
                r, par = PAIR * (pair - 1) + n, n % 2
                src = ps[:, 4 + par, :].rearrange("d (h b s) -> d b h s", h=HPC, b=BPT)
                act.wait_ge(turned, r + 1)
                if kind == "k":
                    wait(act, stored[par], 16 * ((r // 2)))
                    act.copy(kout[:, par, :, :, :], src).then_inc(k_copied, 1)
                else:
                    before = 16 * (K_UNITS // 2) + 32 * (PAIR // 2) * (pair - 2) + 32 * (n // 2)
                    wait(act, stored[par], before)
                    act.copy(qout_h[:, par, :, :, :], src).then_inc(q_hi_copied, 1)

            def body(pair, kind):
                for n in range(PAIR):
                    g, par = PAIR * pair + n, n % 2
                    if kind == 0:
                        act.wait_ge(mm_done, g + 1)
                        wait(act, v_stored[par], 16 * (n // 2))
                        act.copy(vout[:, par, :], ps[:, n % 4, :]).then_inc(v_copied, 1)
                    else:
                        r = PAIR * (pair - 1) + n
                        act.wait_ge(mm_done, g + 1)
                        wait(act, rotated_ready, r - 1)
                        act.copy(proj[:, par, :, :], ps[:, n % 4, :].rearrange("p (h d) -> p h d", h=HPC))\
                           .then_inc(proj_ready, 1)
                        wait(act, ss_ready, r - 1)
                        wait(act, rinv_ready, r - 1)
                        for h in range(HPC):
                            last = act.activation(square[:, par, h, :], ps[:, n % 4, D * h:D * h + D], ACT.Square,
                                                  accum_out=ss[:, par, h:h + 1])
                        last.then_inc(ss_ready, 1)
                    m = n - LAG
                    if rot_kind(kind, m):
                        turned_out(pair, m, rot_kind(kind, m))
                    split_next(pair, n)

            over_pairs(act, body)
            for m in range(-LAG, 0):
                turned_out(PAIRS, m, "q")

        @block.vector
        def _(dve):
            def split_next(pair, n):
                t, c = n % TILES, n // TILES
                if t % 3 == 0 and 3 <= t <= 12:
                    kt, par = t // 3 - 1, (c + 1) % 2
                    dve.wait_ge(w_hi_ready, KT * (2 * pair + c + 1) + kt + 1)
                    dve.tensor_tensor(wl[:, par, kt, :], wraw[:, par, kt, :], wh[:, par, kt, :].bitcast(F32),
                                      ALU.subtract).then_inc(w_lo_ready, 1)

            for kt in range(KT):
                dve.wait_ge(w_hi_ready, kt + 1)
                dve.tensor_tensor(wl[:, 0, kt, :], wraw[:, 0, kt, :], wh[:, 0, kt, :].bitcast(F32),
                                  ALU.subtract).then_inc(w_lo_ready, 1)
            for quarter in range(4):
                dve.wait_ge(x_hi_ready, quarter + 1)
                dve.tensor_tensor(xl[:, quarter, :, :], xstage[:, :, :], xh[:, quarter, :, :].bitcast(F32),
                                  ALU.subtract).then_inc(x_lo_ready, 1)

            done = 0

            def step(instruction):
                nonlocal done
                instruction.then_inc(table_step, 1)
                done += 1
                dve.wait_ge(table_step, done)

            dve.wait_ge(consts_loaded, 80)
            step(dve.tensor_copy(pos[:, :], pos_i[:, :]))
            step(dve.tensor_tensor(pos[:, :], pos[:, :], row_in_seq[:, :].to_broadcast([P, TILES]), ALU.add))
            step(dve.tensor_tensor(angle[:, :, :], pos[:, :].unsqueeze(2).to_broadcast([P, TILES, D // 2]),
                                   inv_freq[:, :].unsqueeze(1).to_broadcast([P, TILES, D // 2]), ALU.mult))
            step(dve.tensor_scalar(turns[:, :, :], angle[:, :, :], float(1 / (2 * np.pi)), None, ALU.mult))
            step(dve.tensor_copy(sine[:, :, :], turns[:, :, :]))
            step(dve.scalar_tensor_tensor(out=angle[:, :, :], in0=sine[:, :, :], scalar=-TWO_PI_1,
                                          in1=angle[:, :, :], op0=ALU.mult, op1=ALU.add))
            step(dve.scalar_tensor_tensor(out=angle[:, :, :], in0=sine[:, :, :], scalar=-TWO_PI_2,
                                          in1=angle[:, :, :], op0=ALU.mult, op1=ALU.add))
            step(dve.scalar_tensor_tensor(out=angle[:, :, :], in0=sine[:, :, :], scalar=-TWO_PI_3,
                                          in1=angle[:, :, :], op0=ALU.mult, op1=ALU.add))
            step(dve.tensor_scalar(angle[:, :, :], angle[:, :, :], PI_BELOW, -PI_BELOW, ALU.min, ALU.max))
            dve.wait_ge(sines_ready, 2)
            step(dve.tensor_tensor(cosine, cosine, cosine, ALU.mult))
            step(dve.tensor_scalar(cosine, cosine, -2.0, 1.0, ALU.mult, ALU.add))
            step(dve.tensor_scalar(norm_w[:, 1, :], norm_w[:, 1, :], -SCALE, None, ALU.mult))
            half = D // 2
            for side in range(2):
                for lo, hi in ((0, half), (half, D)):
                    w_here = norm_w[:, side, lo:hi].unsqueeze(1).to_broadcast([P, TILES, half])
                    step(dve.tensor_tensor(cos_w[:, side, :, lo:hi], cosine, w_here, ALU.mult))
                first = norm_w[:, side, 0:half].unsqueeze(1).to_broadcast([P, TILES, half])
                second = norm_w[:, side, half:D].unsqueeze(1).to_broadcast([P, TILES, half])
                step(dve.tensor_tensor(sin_w[:, side, :, half:D], sine[:, :, :], first, ALU.mult))
                step(dve.scalar_tensor_tensor(out=sin_w[:, side, :, 0:half], in0=sine[:, :, :], scalar=-1.0,
                                              in1=second, op0=ALU.mult, op1=ALU.mult))
            assert done == TABLE_STEPS, done

            def lo_out(pair, n, kind):
                if kind == "k":
                    return
                r, par = PAIR * (pair - 1) + n, n % 2
                src = ps[:, 4 + par, :].rearrange("d (h b s) -> d b h s", h=HPC, b=BPT)
                wait(dve, q_hi_copied, r - K_UNITS + 1)
                dve.tensor_tensor(qout_l[:, par, :, :, :], src, qout_h[:, par, :, :, :].bitcast(F32), ALU.subtract)\
                   .then_inc(q_lo_copied, 1)

            def body(pair, kind):
                for n in range(PAIR):
                    if kind:
                        r, par, t = PAIR * (pair - 1) + n, n % 2, n % TILES
                        side = 0 if kind == 1 else 1
                        dve.wait_ge(proj_ready, r + 1)
                        dve.tensor_tensor(by_cos[:, :, :], proj[:, par, :, :],
                                          cos_w[:, side, t:t + 1, :].to_broadcast([P, HPC, D]), ALU.mult)\
                           .then_inc(by_cos_ready, 1)
                        dve.wait_ge(by_cos_ready, r + 1)
                        dve.wait_ge(by_sin_ready, r + 1)
                        dve.tensor_tensor(rotated[:, :, :], by_cos[:, :, :], by_sin[:, par, :, :], ALU.add)\
                           .then_inc(rotated_ready, 1)
                        dve.wait_ge(rotated_ready, r + 1)
                        dve.wait_ge(rinv_ready, r + 1)
                        wait(dve, turned, r - 1)
                        dve.tensor_tensor(normed[:, par, :, :], rotated[:, :, :],
                                          rinv[:, par, :].unsqueeze(2).to_broadcast([P, HPC, D]), ALU.mult)\
                           .then_inc(normed_ready, 1)
                    m = n - LAG
                    if rot_kind(kind, m):
                        lo_out(pair, m, rot_kind(kind, m))
                    split_next(pair, n)

            over_pairs(dve, body)
            for m in range(-LAG, 0):
                lo_out(PAIRS, m, "q")

        @block.tensor
        def _(pe):
            pe.wait_ge(ident_ready, 2)

            def turn(pair, n, kind):
                r, par = PAIR * (pair - 1) + n, n % 2
                pe.wait_ge(normed_ready, r + 1)
                if isinstance(r, int) and r < K_UNITS + 2:
                    wait(pe, k_copied, r - 1)
                else:
                    wait(pe, q_lo_copied, r - K_UNITS - 1)
                for h in range(HPC):
                    last = pe.transpose(ps[:, 4 + par, P * h:P * h + P], normed[:, par, h, :], ident[:, :])
                last.then_inc(turned, 1)

            def body(pair, kind):
                for n in range(PAIR):
                    g, t, c = PAIR * pair + n, n % TILES, n // TILES
                    if t == 0:
                        pe.wait_ge(w_lo_ready, KT * (2 * pair + c + 1))
                    if kind == 0 and c == 0 and t % 4 == 0:
                        pe.wait_ge(x_lo_ready, t // 4 + 1)
                    if kind == 0 or (kind == 1 and n < 4):
                        wait(pe, v_copied, g - 3)
                    else:
                        wait(pe, ss_ready, g - V_UNITS - 3)
                    cols = slice(P * (t % 4), P * (t % 4) + P)
                    for kt in range(KT):
                        for x_part, w_part in ((xh, wh), (xl, wh), (xh, wl)):
                            last = pe.matmul(ps[:, n % 4, :], x_part[:, t // 4, kt, cols], w_part[:, c, kt, :],
                                             start=(kt == 0 and x_part is xh and w_part is wh),
                                             stop=(kt == KT - 1 and w_part is wl))
                    last.then_inc(mm_done, 1)
                    m = n - LAG
                    if rot_kind(kind, m):
                        turn(pair, m, rot_kind(kind, m))

            over_pairs(pe, body)
            for m in range(-LAG, 0):
                turn(PAIRS, m, "q")


def attend(nc, ps, a, scratch):
    with ExitStack() as ctx:
        def sb(name, shape, dt=F32):
            return ctx.enter_context(nc.sbuf_tensor("a_" + name, shape, dt))

        def sem(name):
            return ctx.enter_context(nc.semaphore("a_" + name))

        RING = 4
        KEY_TILES = CACHED // P + 1
        PADDED = KEY_TILES * P
        HALF_HEADS = HK // 2
        HALF = HALF_HEADS * D
        GATHERS = KEY_TILES - 1
        HALF_KEYS = KEYS // 2
        SETUP_STEPS = 3
        kcache = sb("kcache", [P, PAGES, HK, PSIZE])
        kraw = sb("kraw", [P, 2, NPP + 1, HK, PSIZE])
        khi = sb("khi", [P, RING, KEYS], F32R)
        klo = sb("klo", [P, RING, KEYS], F32R)
        qhi = sb("qhi", [P, 2, HQ * SEQ], F32R)
        qlo = sb("qlo", [P, 2, HQ * SEQ], F32R)
        v = sb("v", [P, 2, KEY_TILES, HALF])
        key_pos = sb("key_pos", [P, KEYS])
        mask = sb("mask", [P, 2, KEYS])
        seqlen_i = sb("seqlen_i", [P, BATCH], I32)
        seqlen = sb("seqlen", [P, BATCH])
        page_of_row = sb("page_of_row", [P, BATCH * GATHERS], I32)
        half_row = sb("half_row", [P, 2])
        vrow = sb("vrow", [P, 2, BATCH * GATHERS], I32)
        vrow_now = sb("vrow_now", [P, 2, 2, GATHERS], I32)
        scores = sb("scores", [P, 2, KEYS])
        nmax = sb("nmax", [P, 2])
        probs = sb("probs", [P, 2, PADDED])
        sums = sb("sums", [P, 4])
        rsum = sb("rsum", [P, 4])
        probsT = sb("probsT", [P, 2, KEY_TILES, P])
        o_rows = sb("o_rows", [P, 2, D])
        oT = sb("oT", [P, 2, HK, REP * SEQ])
        ident = sb("ident", [P, P])

        consts_loaded = sem("consts_loaded")
        kcache_loaded = sem("kcache_loaded")
        kraw_loaded = [sem("kraw_loaded0"), sem("kraw_loaded1")]
        q_loaded = [sem("q_loaded0"), sem("q_loaded1")]
        v_loaded = [sem("v_loaded0"), sem("v_loaded1")]
        v_new_loaded = [sem("v_new_loaded0"), sem("v_new_loaded1")]
        o_stored = [sem("o_stored0"), sem("o_stored1")]
        pool_passed = sem("pool_passed")
        dve_passed = sem("dve_passed")
        ident_ready = sem("ident_ready")
        key_pos_ready = sem("key_pos_ready")
        zeroed = sem("zeroed")
        setup_done = sem("setup_done")
        vrow_now_ready = sem("vrow_now_ready")
        mask_ready = sem("mask_ready")
        k_hi_ready = sem("k_hi_ready")
        k_lo_ready = sem("k_lo_ready")
        qk_done = sem("qk_done")
        scores_masked = sem("scores_masked")
        probs_ready = sem("probs_ready")
        probs_turned = sem("probs_turned")
        probsT_ready = sem("probsT_ready")
        pv_done = sem("pv_done")
        rsum_ready = sem("rsum_ready")
        o_scaled = sem("o_scaled")
        o_turned = sem("o_turned")
        oT_ready = sem("oT_ready")

        PAIR = 2 * HK
        UNITS = BATCH * HK
        block = ctx.enter_context(nc.Block())

        def over_units(eng, step, lag):
            for n in range(PAIR):
                step(0, n)
            with eng.Fori(1, BATCH // 2) as i:
                for n in range(PAIR):
                    step(i, n)
            for n in range(lag):
                step(BATCH // 2, n)

        def there(i, n, total=UNITS):
            return not isinstance(i, int) or 0 <= PAIR * i + n < total

        @block.sync
        def _(sp):
            for part in range(4):
                pages = slice(16 * part, 16 * part + 16)
                sp.dma_start(kcache[:, pages, :, :], a["k_cacheT"][:, pages, :, :]).then_inc(kcache_loaded, 16)
            sp.wait_ge(kcache_loaded, 64)
            page = [sp.alloc_register(f"page{j}") for j in range(NPP)]

            def load_keys(b, par):
                sp.load(page, a["block_table"][bass.ds(b, 1), :])
                wait(sp, k_lo_ready, HK * (b - 1))
                for j in range(NPP):
                    at = sp.snap(page[j], min_val=0, max_val=PAGES - 1)
                    sp.dma_start(kraw[:, par, j, :, :], kcache[:, bass.ds(at, 1), :, :])\
                      .then_inc(kraw_loaded[par], 16)
                sp.dma_start(kraw[:, par, NPP, :, :], scratch["k"][bass.ds(b, 1), :, :, :]
                             .rearrange("o d h s -> d (o h) s")).then_inc(kraw_loaded[par], 16)

            def load_q(b, par):
                wait(sp, qk_done, HK * (b - 1))
                for dst, name in ((qhi, "qh"), (qlo, "ql")):
                    sp.dma_start(dst[:, par, :].bitcast(F32), scratch[name][bass.ds(b, 1), :, :, :]
                                 .rearrange("o d h s -> d (o h s)")).then_inc(q_loaded[par], 16)

            def load_new_v(b, half):
                wait(sp, pv_done, HK * (b - 1) + HALF_HEADS * (half + 1))
                sp.dma_start(v[0:SEQ, half, GATHERS, :],
                             scratch["v"][bass.ds(SEQ * b, SEQ), HALF * half:HALF * half + HALF])\
                  .then_inc(v_new_loaded[half], 16)

            def store(b, par):
                sp.wait_ge(oT_ready, HK * (b + 1))
                sp.dma_start(scratch["o"][bass.ds(b, 1), :, :, :].rearrange("o d h s -> d (o h s)"),
                             oT[:, par, :, :].rearrange("d h q -> d (h q)")).then_inc(o_stored[par], 16)

            def sequence(b, par):
                load_new_v(b, 0)
                if not (isinstance(b, int) and b == BATCH - 1):
                    load_keys(b + 1, 1 - par)
                    load_q(b + 1, 1 - par)
                load_new_v(b, 1)
                if not (isinstance(b, int) and b == 0):
                    store(b - 1, 1 - par)

            load_keys(0, 0)
            load_q(0, 0)
            sp.wait_ge(zeroed, 2)
            sequence(0, 0)
            sequence(1, 1)
            with sp.Fori(1, BATCH // 2 - 1) as i:
                for par in range(2):
                    sequence(sp.snap(2 * i + par), par)
            sequence(BATCH - 2, 0)
            sequence(BATCH - 1, 1)
            store(BATCH - 1, 1)
            for par in range(2):
                sp.wait_ge(o_stored[par], 16 * BATCH // 2)

        @block.gpsimd
        def _(pool):
            pool.dma_start(seqlen_i[:, :], a["seqlen_all"]).then_inc(consts_loaded, 16)
            pool.dma_start(page_of_row[:, :], a["page_of_row"]).then_inc(consts_loaded, 16)
            pool.dma_start(half_row[:, :], a["half_row"]).then_inc(consts_loaded, 16)
            build_identity(pool, ident, ident_ready)
            pool.iota(key_pos[:, 0:CACHED], pattern=[[1, CACHED]], base=0, channel_multiplier=0,
                      allow_small_or_imprecise_dtypes=True).then_inc(key_pos_ready, 1)
            pool.memset(key_pos[:, CACHED:KEYS], -1.0).then_inc(key_pos_ready, 1)
            pool.wait_ge(setup_done, SETUP_STEPS)

            def gather(b, par):
                for half in range(2):
                    wait(pool, v_loaded[half], 16 * GATHERS * (b - 1))
                pool.tensor_copy(vrow_now[:, par, :, :], vrow[:, :, bass.ds(GATHERS * b, GATHERS)])\
                    .then_inc(vrow_now_ready, 1)
                wait_all(pool, pool_passed, (vrow_now_ready, b + 1))
                for half in range(2):
                    wait_all(pool, pool_passed, (pv_done, HK * (b - 1) + HALF_HEADS * (half + 1)))
                    for j in range(GATHERS):
                        pool.indirect_dma_start(
                            v[:, half, j, :], None, a["v_rows"],
                            bass.IndirectOffsetOnAxis(ap=vrow_now[:, par, half, j:j + 1], axis=0))\
                            .then_inc(v_loaded[half], 16)

            gather(0, 0)
            gather(1, 1)
            with pool.Fori(1, BATCH // 2) as i:
                for par in range(2):
                    gather(pool.snap(2 * i + par), par)

        @block.scalar
        def _(act):
            def split_high(i, n):
                u, par = PAIR * i + n, n // HK
                if n % HK == 0:
                    act.wait_ge(kraw_loaded[par], 16 * (NPP + 1) * (i + 1))
                wait(act, qk_done, u - RING + 1)
                act.copy(khi[:, n % RING, :].rearrange("d (j s) -> d j s", s=PSIZE), kraw[:, par, :, n % HK, :])\
                   .then_inc(k_hi_ready, 1)

            def exponentials(i, n):
                u, par = PAIR * i + n, n % 2
                act.wait_ge(scores_masked, u + 1)
                wait(act, probs_turned, u - 1)
                wait(act, rsum_ready, u - 3)
                act.activation(probs[:, par, 0:KEYS], scores[:, par, :], ACT.Exp, bias=nmax[:, par:par + 1],
                               scale=-1.0, accum_out=sums[:, n % 4:n % 4 + 1]).then_inc(probs_ready, 1)

            def turned_out(i, n):
                u, par = PAIR * i + n, n % 2
                act.wait_ge(probs_turned, u + 1)
                wait(act, pv_done, u - 1)
                act.copy(probsT[:, par, :, :].rearrange("k j q -> k (j q)"),
                         ps[:, 4:6, :].rearrange("k a q -> k (a q)")[:, 0:PADDED]).then_inc(probsT_ready, 1)

            act.wait_ge(zeroed, 2)

            def step(i, n):
                if there(i, n - 4):
                    turned_out(i, n - 4)
                if there(i, n - 3):
                    exponentials(i, n - 3)
                if there(i, n):
                    split_high(i, n)

            over_units(act, step, 4)

        @block.vector
        def _(dve):
            dve.memset(v[:, :, GATHERS, :], 0.0).then_inc(zeroed, 1)
            dve.memset(probs[:, :, KEYS:PADDED], 0.0).then_inc(zeroed, 1)
            dve.wait_ge(consts_loaded, 48)
            dve.tensor_copy(seqlen[:, :], seqlen_i[:, :]).then_inc(setup_done, 1)
            for half in range(2):
                dve.tensor_scalar(vrow[:, half, :], page_of_row[:, :], float(2 * PSIZE), half_row[:, half:half + 1],
                                  ALU.mult, ALU.add).then_inc(setup_done, 1)
            dve.wait_ge(setup_done, SETUP_STEPS)
            dve.wait_ge(key_pos_ready, 2)

            def make_mask(i, n):
                b, par = 2 * i + n // HK, n // HK
                dve.tensor_scalar(mask[:, par, :], key_pos[:, :], seqlen[:, bass.ds(b, 1)], MASKED,
                                  ALU.is_ge, ALU.mult).then_inc(mask_ready, 1)

            def split_low(i, n):
                u, par = PAIR * i + n, (n // HK) % 2
                dve.wait_ge(k_hi_ready, u + 1)
                dve.tensor_tensor(klo[:, n % RING, :].rearrange("d (j s) -> d j s", s=PSIZE),
                                  kraw[:, par, :, n % HK, :],
                                  khi[:, n % RING, :].bitcast(F32).rearrange("d (j s) -> d j s", s=PSIZE),
                                  ALU.subtract).then_inc(k_lo_ready, 1)

            def mask_scores(i, n):
                u, par = PAIR * i + n, n % 2
                wait_all(dve, dve_passed, (qk_done, u + 1), (mask_ready, 2 * i + n // HK + 1),
                         (probs_ready, u - 1))
                dve.tensor_tensor_reduce(scores[:, par, :].rearrange("q (a k) -> q a k", a=2),
                                         ps[:, 2 * par:2 * par + 2, 0:HALF_KEYS],
                                         mask[:, (n // HK) % 2, :].rearrange("q (a k) -> q a k", a=2),
                                         1.0, 0.0 + 3e38, ALU.add, ALU.min, nmax[:, par:par + 1])\
                   .then_inc(scores_masked, 1)

            def invert_sum(i, n):
                u = PAIR * i + n
                dve.wait_ge(probs_ready, u + 1)
                dve.reciprocal(rsum[:, n % 4:n % 4 + 1], sums[:, n % 4:n % 4 + 1]).then_inc(rsum_ready, 1)

            def scale_out(i, n):
                u, par = PAIR * i + n, n % 2
                dve.wait_ge(rsum_ready, u + 1)
                dve.wait_ge(pv_done, u + 1)
                wait(dve, o_turned, u - 1)
                dve.tensor_scalar(o_rows[:, par, :], ps[:, 6, 0:D], rsum[:, n % 4:n % 4 + 1], None, ALU.mult)\
                   .then_inc(o_scaled, 1)

            def turned_out(i, n):
                u, par = PAIR * i + n, (n // HK) % 2
                if n % HK == 0:
                    wait(dve, o_stored[par], 16 * (i + n // PAIR))
                dve.wait_ge(o_turned, u + 1)
                dve.tensor_copy(oT[:, par, n % HK, :], ps[:, 7, 0:P]).then_inc(oT_ready, 1)

            def step(i, n):
                if there(i, n) and n % HK == 0:
                    make_mask(i, n)
                if there(i, n - 3):
                    mask_scores(i, n - 3)
                if there(i, n - 1):
                    split_low(i, n - 1)
                if there(i, n - 5):
                    invert_sum(i, n - 5)
                    scale_out(i, n - 5)
                if there(i, n - 6):
                    turned_out(i, n - 6)

            over_units(dve, step, 6)

        @block.tensor
        def _(pe):
            pe.wait_ge(ident_ready, 2)

            def score(i, n):
                u, par, b_par, h = PAIR * i + n, n % 2, n // HK, n % HK
                if h == 0:
                    pe.wait_ge(q_loaded[b_par], 32 * (i + 1))
                pe.wait_ge(k_lo_ready, u + 1)
                wait(pe, scores_masked, u - 1)
                q_cols = slice(P * h, P * h + P)
                for part in range(2):
                    keys = slice(HALF_KEYS * part, HALF_KEYS * part + HALF_KEYS)
                    out = ps[:, 2 * par + part, 0:HALF_KEYS]
                    pe.matmul(out, qhi[:, b_par, q_cols], khi[:, n % RING, keys], start=True, stop=False)
                    pe.matmul(out, qhi[:, b_par, q_cols], klo[:, n % RING, keys], start=False, stop=False)
                    last = pe.matmul(out, qlo[:, b_par, q_cols], khi[:, n % RING, keys], start=False, stop=True)
                last.then_inc(qk_done, 1)

            def turn_probs(i, n):
                u, par = PAIR * i + n, n % 2
                pe.wait_ge(probs_ready, u + 1)
                wait(pe, probsT_ready, u)
                for j in range(KEY_TILES):
                    last = pe.transpose(ps[:, 4 + j // 4, P * (j % 4):P * (j % 4) + P],
                                        probs[:, par, P * j:P * j + P], ident[:, :])
                last.then_inc(probs_turned, 1)

            def weigh(i, n):
                u, par, half = PAIR * i + n, n % 2, (n % HK) // HALF_HEADS
                if n % HALF_HEADS == 0:
                    pe.wait_ge(v_loaded[half], 16 * GATHERS * (2 * i + n // HK + 1))
                    pe.wait_ge(v_new_loaded[half], 16 * (2 * i + n // HK + 1))
                pe.wait_ge(probsT_ready, u + 1)
                wait(pe, o_scaled, u)
                cols = slice(D * (n % HALF_HEADS), D * (n % HALF_HEADS) + D)
                for j in range(KEY_TILES):
                    last = pe.matmul(ps[:, 6, 0:D], probsT[:, par, j, :], v[:, half, j, cols],
                                     start=(j == 0), stop=(j == KEY_TILES - 1))
                last.then_inc(pv_done, 1)

            def turn_out(i, n):
                u, par = PAIR * i + n, n % 2
                pe.wait_ge(o_scaled, u + 1)
                wait(pe, oT_ready, u)
                pe.transpose(ps[:, 7, 0:P], o_rows[:, par, :], ident[:, :]).then_inc(o_turned, 1)

            def step(i, n):
                if there(i, n):
                    score(i, n)
                if there(i, n - 1):
                    turn_probs(i, n - 1)
                if there(i, n - 2):
                    weigh(i, n - 2)
                if there(i, n - 3):
                    turn_out(i, n - 3)

            over_units(pe, step, 3)


def finish(nc, ps, a, scratch, out):
    with ExitStack() as ctx:
        def sb(name, shape, dt=F32):
            return ctx.enter_context(nc.sbuf_tensor("f_" + name, shape, dt))

        def sem(name):
            return ctx.enter_context(nc.semaphore("f_" + name))

        QUARTER = HQ // 8
        CHUNKS = HQ // QUARTER
        G = BPT * RANK
        stage = sb("stage", [P, 2, HID])
        woh = sb("woh", [P, HQ, HID], F32R)
        wol = sb("wol", [P, HQ, HID], F32R)
        bwh = sb("bwh", [P, 2, KT, HID], F32R)
        bwl = sb("bwl", [P, 2, KT, HID], F32R)
        o_raw = sb("o_raw", [P, 2, BPT, QUARTER, SEQ])
        oh = sb("oh", [P, 2, QUARTER, P], F32R)
        ol = sb("ol", [P, 2, QUARTER, P], F32R)
        x_in = sb("x_in", [P, 2, HID])
        x_now = sb("x_now", [P, 2, HID])
        xT = sb("xT", [P, KT, P])
        xTh = sb("xTh", [P, KT, P], F32R)
        xTl = sb("xTl", [P, KT, P], F32R)
        down = sb("down", [G, 3, HID])
        downT = sb("downT", [P, KT, G])
        up = sb("up", [P, 3, HID])
        hidden = sb("hidden", [P, P])
        own = sb("own", [G, P])
        ident = sb("ident", [P, P])
        adapter = sb("adapter", [G, 3, TILES], I32)
        rank_row = sb("rank_row", [G, 1])
        row = sb("row", [G, 3, TILES], I32)
        row_now = sb("row_now", [G, 2, 3], I32)

        consts_loaded = sem("consts_loaded")
        stage_loaded = sem("stage_loaded")
        w_hi_ready = sem("w_hi_ready")
        w_lo_ready = sem("w_lo_ready")
        bias_loaded = sem("bias_loaded")
        zeroed = sem("zeroed")
        pool_passed = sem("pool_passed")
        pe_passed = sem("pe_passed")
        ident_ready = sem("ident_ready")
        own_ready = sem("own_ready")
        row_ready = sem("row_ready")
        row_now_ready = sem("row_now_ready")
        adapters_loaded = [sem(f"adapters_loaded{layer}") for layer in range(3)]
        x_loaded = [sem("x_loaded0"), sem("x_loaded1")]
        o_loaded = [sem("o_loaded0"), sem("o_loaded1")]
        o_hi_ready = sem("o_hi_ready")
        o_lo_ready = sem("o_lo_ready")
        o_used = sem("o_used")
        x1_ready = sem("x1_ready")
        x_turned = sem("x_turned")
        down_turned = sem("down_turned")
        xT_ready = sem("xT_ready")
        xTh_ready = sem("xTh_ready")
        xTl_ready = sem("xTl_ready")
        downT_ready = sem("downT_ready")
        hidden_done = sem("hidden_done")
        hidden_ready = sem("hidden_ready")
        layer_done = sem("layer_done")
        x_ready = sem("x_ready")
        out_stored = sem("out_stored")

        WO_PIECES = HQ // 2
        PIECES = WO_PIECES + 2 * KT // 2

        def piece(p, high):
            if p < WO_PIECES:
                return (woh if high else wol)[:, 2 * p:2 * p + 2, :]
            p -= WO_PIECES
            return (bwh if high else bwl)[:, p // 2, 2 * (p % 2):2 * (p % 2) + 2, :]

        TURN_SLOT = {0: 0, 2: 1, 5: 2}
        HIDDEN_SLOT = {1: 0, 3: 1, 6: 2}
        END_SLOT = {1: 0, 4: 1, 6: 2}
        HAS_BASE = {0: 0, 2: 1}
        block = ctx.enter_context(nc.Block())

        def over_tiles(eng, tile):
            tile(0, 0)
            tile(1, 1)
            with eng.Fori(1, TILES // 2 - 1) as i:
                for par in range(2):
                    tile(eng.snap(2 * i + par), par)
            tile(TILES - 2, 0)
            tile(TILES - 1, 1)

        def is_number(t, number):
            return isinstance(t, int) and t == number

        def o_chunk(t, c):
            return scratch["o"][bass.ds(BPT * t, BPT), :, QUARTER * c:QUARTER * c + QUARTER, :]\
                .rearrange("b d h s -> d b (h s)")

        def as_loaded(buffer, par):
            return buffer[:, par, :, :, :].rearrange("d b h s -> d b (h s)")

        @block.sync
        def _(sp):
            sp.dma_start(x_in[:, 0, :], a["x"][0:P, :]).then_inc(x_loaded[0], 16)
            for c in range(2):
                sp.dma_start(as_loaded(o_raw, c), o_chunk(0, c)).then_inc(o_loaded[c], 16)
            for p in range(PIECES):
                wait(sp, w_lo_ready, p)
                src = a["woT"][:, 2 * p:2 * p + 2, :] if p < WO_PIECES else \
                    a["baseT"][:, (p - WO_PIECES) // 2, 2 * (p % 2):2 * (p % 2) + 2, :]
                sp.dma_start(stage[:, :, :], src).then_inc(stage_loaded, 16)
            sp.wait_ge(zeroed, 4)
            for layer, name in ((0, "bias1"), (2, "bias3")):
                sp.dma_start(up[G:G + 1, layer, :], a[name]).then_inc(bias_loaded, 16)

            def tile(t, par):
                for c in range(CHUNKS):
                    if not (is_number(t, TILES - 1) and c + 2 >= CHUNKS):
                        sp.wait_ge(o_lo_ready, CHUNKS * t + c + 1)
                        ahead = (t, c + 2) if c + 2 < CHUNKS else (t + 1, c + 2 - CHUNKS)
                        sp.dma_start(as_loaded(o_raw, c % 2), o_chunk(*ahead)).then_inc(o_loaded[c % 2], 16)
                    if c == 3 and not is_number(t, TILES - 1):
                        wait(sp, x1_ready, t)
                        sp.dma_start(x_in[:, 1 - par, :], a["x"][bass.ds(P * t + P, P), :])\
                          .then_inc(x_loaded[1 - par], 16)
                if not is_number(t, 0):
                    put(t - 1)

            def put(t):
                sp.wait_ge(x_ready, 3 * (t + 1))
                sp.dma_start(out[bass.ds(P * t, P), :], x_now[:, 1, :]).then_inc(out_stored, 16)

            over_tiles(sp, tile)
            put(TILES - 1)
            sp.wait_ge(out_stored, 16 * TILES)

        @block.gpsimd
        def _(pool):
            pool.dma_start(adapter[:, :, :], a["adapter_by_tile"]).then_inc(consts_loaded, 16)
            pool.dma_start(rank_row[:, :], a["rank_row"]).then_inc(consts_loaded, 16)
            pool.dma_start(own[:, :], a["own"]).then_inc(own_ready, 16)
            build_identity(pool, ident, ident_ready)
            pool.wait_ge(row_ready, 1)

            def gather(t, par):
                for layer in range(3):
                    wait(pool, adapters_loaded[layer], 32 * (t - 1))
                pool.tensor_copy(row_now[:, par, :], row[:, :, bass.ds(t, 1)].rearrange("g l o -> g (l o)"))\
                    .then_inc(row_now_ready, 1)
                wait_all(pool, pool_passed, (row_now_ready, t + 1))
                for layer in range(3):
                    wait_all(pool, pool_passed, (layer_done, 3 * (t - 1) + layer + 1))
                    for dst, name in ((down, "down"), (up, "up")):
                        pool.indirect_dma_start(
                            dst[0:G, layer, :], None, a[f"{name}{layer + 1}"],
                            bass.IndirectOffsetOnAxis(ap=row_now[:, par, layer:layer + 1], axis=0))\
                            .then_inc(adapters_loaded[layer], 16)

            over_tiles(pool, gather)

        @block.scalar
        def _(act):
            for p in range(PIECES):
                act.wait_ge(stage_loaded, 16 * (p + 1))
                act.copy(piece(p, True), stage[:, :, :]).then_inc(w_hi_ready, 1)

            def split_high(t, c):
                n, par = CHUNKS * t + c, c % 2
                act.wait_ge(o_loaded[par], 16 * (CHUNKS // 2 * t + c // 2 + 1))
                wait(act, o_used, n - 1)
                act.copy(oh[:, par, :, :].rearrange("d h (b s) -> d h b s", b=BPT),
                         o_raw[:, par, :, :, :].rearrange("d b h s -> d h b s")).then_inc(o_hi_ready, 1)

            def chain(t, c):
                if c in TURN_SLOT:
                    k = 3 * t + TURN_SLOT[c]
                    turned = ps[:, 2, :].rearrange("i (k r) -> i k r", k=KT)
                    act.wait_ge(x_turned, k + 1)
                    wait(act, layer_done, k)
                    if TURN_SLOT[c] in HAS_BASE:
                        act.copy(xTh[:, :, :], turned).then_inc(xTh_ready, 1)
                    act.copy(xT[:, :, :], turned).then_inc(xT_ready, 1)
                    act.wait_ge(down_turned, k + 1)
                    act.copy(downT[:, :, :], ps[:, 3, 0:KT * G].rearrange("i (k g) -> i k g", k=KT))\
                       .then_inc(downT_ready, 1)

            def tile(t, par):
                for c in range(CHUNKS):
                    if c + 1 < CHUNKS:
                        split_high(t, c + 1)
                    elif not is_number(t, TILES - 1):
                        split_high(t + 1, 0)
                    if not is_number(t, 0):
                        chain(t - 1, c)

            split_high(0, 0)
            over_tiles(act, tile)
            for c in range(CHUNKS):
                chain(TILES - 1, c)

        @block.vector
        def _(dve):
            dve.memset(up[G:P, :, :], 0.0).then_inc(zeroed, 1)
            dve.memset(hidden[G:P, :], 0.0).then_inc(zeroed, 1)
            dve.memset(hidden[0:G, :], 0.0).then_inc(zeroed, 1)
            dve.wait_ge(zeroed, 3)
            dve.memset(hidden[G:G + 1, :], 1.0).then_inc(zeroed, 1)
            dve.wait_ge(consts_loaded, 32)
            dve.tensor_scalar(row[:, :, :], adapter[:, :, :], float(RANK), rank_row[:, 0:1], ALU.mult, ALU.add)\
               .then_inc(row_ready, 1)
            for p in range(PIECES):
                dve.wait_ge(w_hi_ready, p + 1)
                dve.tensor_tensor(piece(p, False), stage[:, :, :], piece(p, True).bitcast(F32), ALU.subtract)\
                   .then_inc(w_lo_ready, 1)
            dve.wait_ge(own_ready, 16)

            def split_low(t, c):
                n, par = CHUNKS * t + c, c % 2
                dve.wait_ge(o_hi_ready, n + 1)
                dve.tensor_tensor(ol[:, par, :, :].rearrange("d h (b s) -> d h b s", b=BPT),
                                  o_raw[:, par, :, :, :].rearrange("d b h s -> d h b s"),
                                  oh[:, par, :, :].bitcast(F32).rearrange("d h (b s) -> d h b s", b=BPT),
                                  ALU.subtract).then_inc(o_lo_ready, 1)

            def chain(t, c):
                if c in TURN_SLOT and TURN_SLOT[c] in HAS_BASE:
                    k = 3 * t + TURN_SLOT[c]
                    dve.wait_ge(xTh_ready, 2 * t + HAS_BASE[TURN_SLOT[c]] + 1)
                    dve.wait_ge(xT_ready, k + 1)
                    dve.tensor_tensor(xTl[:, :, :], ps[:, 2, :].rearrange("i (k r) -> i k r", k=KT),
                                      xTh[:, :, :].bitcast(F32), ALU.subtract).then_inc(xTl_ready, 1)
                if c in HIDDEN_SLOT:
                    layer = HIDDEN_SLOT[c]
                    k = 3 * t + layer
                    dve.wait_ge(hidden_done, k + 1)
                    wait(dve, layer_done, k)
                    dve.scalar_tensor_tensor(out=hidden[0:G, :], in0=ps[0:G, 4, 0:P],
                                             scalar=LORA_SCALE if layer == 2 else 1.0, in1=own[:, :],
                                             op0=ALU.mult, op1=ALU.mult).then_inc(hidden_ready, 1)
                if c in END_SLOT:
                    layer = END_SLOT[c]
                    k = 3 * t + layer
                    if layer == 0:
                        wait(dve, out_stored, 16 * t)
                        dve.wait_ge(x1_ready, t + 1)
                    else:
                        dve.wait_ge(x_ready, k)
                    dve.wait_ge(layer_done, k + 1)
                    dve.tensor_tensor(x_now[:, (layer + 1) % 2, :], x_now[:, layer % 2, :], ps[:, 5 + layer, :],
                                      ALU.add).then_inc(x_ready, 1)

            def tile(t, par):
                for c in range(CHUNKS):
                    if c + 1 < CHUNKS:
                        split_low(t, c + 1)
                    elif not is_number(t, TILES - 1):
                        split_low(t + 1, 0)
                    if not is_number(t, 0):
                        chain(t - 1, c)
                dve.wait_ge(x_loaded[par], 16 * (t_pair(dve, t) + 1))
                dve.wait_ge(o_used, CHUNKS * (t + 1))
                wait(dve, x_ready, 3 * t)
                dve.tensor_tensor(x_now[:, 0, :], x_in[:, par, :], ps[:, par, :], ALU.add).then_inc(x1_ready, 1)

            def t_pair(eng, t):
                return t // 2

            split_low(0, 0)
            over_tiles(dve, tile)
            for c in range(CHUNKS):
                chain(TILES - 1, c)

        @block.tensor
        def _(pe):
            pe.wait_ge(ident_ready, 2)
            pe.wait_ge(zeroed, 4)
            pe.wait_ge(w_lo_ready, PIECES)
            pe.wait_ge(bias_loaded, 32)

            def project_chunk(t, par, c):
                pe.wait_ge(o_lo_ready, CHUNKS * t + c + 1)
                if c == 0:
                    wait(pe, x1_ready, t - 1)
                for h in range(QUARTER):
                    for o_part, w_part in ((oh, woh), (ol, woh), (oh, wol)):
                        last = pe.matmul(ps[:, par, :], o_part[:, c % 2, h, :], w_part[:, QUARTER * c + h, :],
                                         start=(c == 0 and h == 0 and o_part is oh and w_part is woh),
                                         stop=(c == CHUNKS - 1 and h == QUARTER - 1 and w_part is wol))
                last.then_inc(o_used, 1)

            def chain(t, c):
                if c in TURN_SLOT:
                    layer = TURN_SLOT[c]
                    k = 3 * t + layer
                    if layer == 0:
                        pe.wait_ge(x1_ready, t + 1)
                    else:
                        pe.wait_ge(x_ready, k)
                    wait(pe, xT_ready, k)
                    wait(pe, xTl_ready, 2 * t + (layer + 1) // 2)
                    for kt in range(KT):
                        last = pe.transpose(ps[:, 2, P * kt:P * kt + P],
                                            x_now[:, layer % 2, P * kt:P * kt + P], ident[:, :])
                    last.then_inc(x_turned, 1)
                    wait_all(pe, pe_passed, (adapters_loaded[layer], 32 * (t + 1)), (downT_ready, k))
                    for kt in range(KT):
                        last = pe.transpose(ps[:, 3, G * kt:G * kt + G], down[:, layer, P * kt:P * kt + P],
                                            ident[0:G, 0:G])
                    last.then_inc(down_turned, 1)
                if c in HIDDEN_SLOT:
                    layer = HIDDEN_SLOT[c]
                    k = 3 * t + layer
                    pe.wait_ge(xT_ready, k + 1)
                    pe.wait_ge(downT_ready, k + 1)
                    wait(pe, hidden_ready, k)
                    for kt in range(KT):
                        last = pe.matmul(ps[0:G, 4, 0:P], downT[:, kt, :], xT[:, kt, :],
                                         start=(kt == 0), stop=(kt == KT - 1))
                    last.then_inc(hidden_done, 1)
                    if layer in HAS_BASE:
                        base = HAS_BASE[layer]
                        wait(pe, x_ready, k - 2)
                        pe.wait_ge(xTl_ready, 2 * t + base + 1)
                        for kt in range(KT):
                            for x_part, w_part in ((xTh, bwh), (xTl, bwh), (xTh, bwl)):
                                pe.matmul(ps[:, 5 + layer, :], x_part[:, kt, :], w_part[:, base, kt, :],
                                          start=(kt == 0 and x_part is xTh and w_part is bwh), stop=False)
                if c in END_SLOT:
                    layer = END_SLOT[c]
                    k = 3 * t + layer
                    pe.wait_ge(hidden_ready, k + 1)
                    pe.matmul(ps[:, 5 + layer, :], hidden[:, :], up[:, layer, :],
                              start=(layer not in HAS_BASE), stop=True).then_inc(layer_done, 1)

            def tile(t, par):
                for c in range(CHUNKS):
                    project_chunk(t, par, c)
                    if not is_number(t, 0):
                        chain(t - 1, c)

            over_tiles(pe, tile)
            for c in range(CHUNKS):
                chain(TILES - 1, c)


def build(nc, a, out):
    scratch = {
        "k": nc.dram_tensor("k_scratch", (BATCH, D, HK, SEQ), F32, kind="Internal").ap(),
        "v": nc.dram_tensor("v_scratch", (TOKENS, HK * D), F32, kind="Internal").ap(),
        "qh": nc.dram_tensor("qh_scratch", (BATCH, D, HQ, SEQ), F32, kind="Internal").ap(),
        "ql": nc.dram_tensor("ql_scratch", (BATCH, D, HQ, SEQ), F32, kind="Internal").ap(),
        "o": nc.dram_tensor("o_scratch", (BATCH, D, HQ, SEQ), F32, kind="Internal").ap(),
    }
    with nc.psum_tensor("banks", [P, 8, 512], F32) as ps:
        project(nc, ps, a, scratch)
        attend(nc, ps, a, scratch)
        finish(nc, ps, a, scratch, out)


def lay_out(x, itok_Bx16_0_63, itok_B_207_1644, itok_B_6_15, itok_B_3_7, itok_B_0_23, L0_cond_Wq, L0_cond_Wk,
            L0_cond_Wv, L0_cond_Wo, L0_cond_q_norm_w, L0_cond_k_norm_w, L0_cond_k_cache, L0_cond_v_cache,
            L1_cond_base_weight, L1_cond_base_bias, L1_cond_lora_A_w, L1_cond_lora_B_w, L2_cond_A, L2_cond_B,
            L3_cond_W, L3_cond_b, L3_cond_lora_As, L3_cond_lora_Bs):
    def by_k(w):
        return w.T.reshape(KT, P, -1).transpose(1, 0, 2)

    w_all = np.concatenate([L0_cond_Wv, L0_cond_Wk, L0_cond_Wq, L0_cond_Wv[:CH]])
    tile_of = np.arange(P) // SEQ
    flat_x = x.reshape(TOKENS, HID)
    seqlen = itok_B_207_1644
    adapters = np.stack([itok_B_6_15, itok_B_3_7, itok_B_0_23])
    return {
        "x": flat_x,
        "xT": flat_x.T.reshape(KT, P, 4, 512).transpose(1, 2, 0, 3),
        "w_all": w_all.reshape(-1, CH, KT, P).transpose(0, 3, 2, 1),
        "seqlen_by_tile": seqlen.reshape(TILES, BPT).T[tile_of],
        "seqlen_all": np.broadcast_to(seqlen, (P, BATCH)),
        "row_in_seq": (np.arange(P) % SEQ).astype(np.float32).reshape(P, 1),
        "inv_freq": np.broadcast_to(
            (np.float32(1) / np.float32(THETA) ** (np.arange(0, D, 2, dtype=np.float32) / np.float32(D)))
            .astype(np.float32), (P, D // 2)),
        "k_norm": np.broadcast_to(L0_cond_k_norm_w, (P, D)),
        "q_norm": np.broadcast_to(L0_cond_q_norm_w, (P, D)),
        "k_cacheT": L0_cond_k_cache.transpose(3, 0, 2, 1),
        "v_rows": L0_cond_v_cache.reshape(PAGES * PSIZE * 2, HK * D // 2),
        "block_table": itok_Bx16_0_63,
        "page_of_row": itok_Bx16_0_63.reshape(BATCH, CACHED // P, BPT)[:, :, tile_of].transpose(2, 0, 1)
        .reshape(P, BATCH * CACHED // P),
        "half_row": (2 * (np.arange(P) % PSIZE)[:, None] + np.arange(2)[None, :]).astype(np.float32),
        "woT": L0_cond_Wo.T.reshape(HQ, D, HID).transpose(1, 0, 2),
        "baseT": np.stack([by_k(L1_cond_base_weight), by_k(L3_cond_W)], axis=1),
        "bias1": L1_cond_base_bias.reshape(1, HID),
        "bias3": L3_cond_b.reshape(1, HID),
        "down1": L1_cond_lora_A_w.reshape(-1, HID),
        "up1": L1_cond_lora_B_w.transpose(0, 2, 1).reshape(-1, HID),
        "down2": L2_cond_B.reshape(-1, HID),
        "up2": L2_cond_A.transpose(0, 2, 1).reshape(-1, HID),
        "down3": L3_cond_lora_As.transpose(0, 2, 1).reshape(-1, HID),
        "up3": L3_cond_lora_Bs.reshape(-1, HID),
        "adapter_by_tile": adapters.reshape(3, TILES, BPT)[:, :, np.arange(BPT * RANK) // RANK].transpose(2, 0, 1),
        "rank_row": (np.arange(BPT * RANK) % RANK).astype(np.float32).reshape(-1, 1),
        "own": (np.arange(BPT * RANK)[:, None] // RANK == np.arange(P)[None, :] // SEQ).astype(np.float32),
    }


def kernel(**inputs):
    import concourse.bacc as bacc
    from concourse.bass_utils import run_bass_kernel_spmd

    nc = bacc.Bacc("TRN2", target_bir_lowering=False, num_devices=1)
    arrays, aps = {}, {}
    for name, value in lay_out(**{k: np.asarray(v) for k, v in inputs.items()}).items():
        arrays[f"in_{name}"] = value = np.ascontiguousarray(value)
        aps[name] = nc.dram_tensor(f"in_{name}", value.shape, mybir.dt.from_np(value.dtype),
                                   kind="ExternalInput").ap()
    out = nc.dram_tensor("out_x", (TOKENS, HID), F32, kind="ExternalOutput").ap()
    build(nc, aps, out)
    result = run_bass_kernel_spmd(nc, [arrays], core_ids=[0])
    return result.results[0]["out_x"].reshape(BATCH, SEQ, HID)
```

```python
from contextlib import ExitStack

import numpy as np

import concourse.bass as bass
from concourse import mybir

F32 = mybir.dt.float32
F32R = mybir.dt.float32r
I32 = mybir.dt.int32
ALU = mybir.AluOpType
ACT = mybir.ActivationFunctionType

P = 128
BATCH, SEQ, HID = 64, 32, 512
D, HQ, HK = 128, 32, 8
REP = HQ // HK
PAGES, PSIZE, NPP = 64, 32, 16
CACHED = NPP * PSIZE
KEYS = CACHED + SEQ
TOKENS = BATCH * SEQ
TILES = TOKENS // P
BPT = P // SEQ
KT = HID // P
CH = 512
HPC = CH // D
V_CHUNKS = HK * D // CH
K_CHUNKS = HK * D // CH
Q_CHUNKS = HQ * D // CH
THETA, EPS = 10000.0, 1e-6
SCALE = 1.0 / float(np.sqrt(D))
MASKED = 1e30
RANK = 16
LORA_SCALE = 2.0
PI_BELOW = float(np.nextafter(np.float32(np.pi), np.float32(0)))
TWO_PI_1 = 6.28125
TWO_PI_2 = 0.0019340515136718750
TWO_PI_3 = float(np.float64(2 * np.pi) - TWO_PI_1 - TWO_PI_2)
ANGLE_STEPS = 9
TABLE_STEPS = 20
X_PIECES = 8
X_STAGES = 4
X_COLS = TOKENS // X_PIECES
X_TILES = X_COLS // P


def wait(eng, sem, count):
    if isinstance(count, int) and count <= 0:
        return
    eng.wait_ge(sem, count)


def wait_all(eng, passed, *waits):
    for sem, count in waits:
        wait(eng, sem, count)
    eng.sem_inc(passed, 1)


def build_identity(eng, ident, ready):
    eng.memset(ident[:, :], 0.0).then_inc(ready, 1)
    eng.wait_ge(ready, 1)
    eng.affine_select(out=ident[:, :], in_=ident[:, :], compare_op=ALU.not_equal, fill=1.0,
                      base=0, pattern=[[-1, P]], channel_multiplier=1).then_inc(ready, 1)


def project(nc, ps, a, scratch):
    with ExitStack() as ctx:
        def sb(name, shape, dt=F32):
            return ctx.enter_context(nc.sbuf_tensor("p_" + name, shape, dt))

        def sem(name):
            return ctx.enter_context(nc.semaphore("p_" + name))

        xstage = sb("xstage", [P, X_STAGES, KT, X_COLS])
        xh = sb("xh", [P, X_PIECES, KT, X_COLS], F32R)
        xl = sb("xl", [P, X_PIECES, KT, X_COLS], F32R)
        wraw = sb("wraw", [P, 2, KT, CH])
        wh = sb("wh", [P, 2, KT, CH], F32R)
        wl = sb("wl", [P, 2, KT, CH], F32R)
        ident = sb("ident", [P, P])
        pos_i = sb("pos_i", [P, TILES], I32)
        pos = sb("pos", [P, TILES])
        row_in_seq = sb("row_in_seq", [P, 1])
        inv_freq = sb("inv_freq", [P, D // 2])
        norm_w = sb("norm_w", [P, 2, D])
        angle = sb("angle", [P, TILES, D // 2])
        turns = sb("turns", [P, TILES, D // 2], I32)
        sine = sb("sine", [P, TILES, D // 2])
        cosine = turns[:, :, :].bitcast(F32)
        cos_w = sb("cos_w", [P, 2, TILES, D])
        sin_w = sb("sin_w", [P, 2, TILES, D])
        proj = sb("proj", [P, 2, HPC, D])
        square = sb("square", [P, 2, HPC, D])
        ss = sb("ss", [P, 2, HPC])
        mean_sq = sb("mean_sq", [P, 2, HPC])
        minus_half = sb("minus_half", [P, HPC])
        rinv = sb("rinv", [P, 2, HPC])
        by_cos = sb("by_cos", [P, HPC, D])
        by_sin = sb("by_sin", [P, 2, HPC, D])
        rotated = sb("rotated", [P, HPC, D])
        normed = sb("normed", [P, 2, HPC, D])
        vout = sb("vout", [P, 2, CH])
        rot_out = sb("rot_out", [P, 2, BPT, HPC, SEQ])

        consts_loaded = sem("consts_loaded")
        x_loaded = [sem(f"x_loaded{i}") for i in range(X_STAGES)]
        x_hi_ready = sem("x_hi_ready")
        x_lo_ready = sem("x_lo_ready")
        w_loaded = [sem("w_loaded0"), sem("w_loaded1")]
        w_hi_ready = sem("w_hi_ready")
        w_lo_ready = sem("w_lo_ready")
        ident_ready = sem("ident_ready")
        table_step = sem("table_step")
        sines_ready = sem("sines_ready")
        mm_done = sem("mm_done")
        v_copied = sem("v_copied")
        v_stored = [sem("v_stored0"), sem("v_stored1")]
        proj_ready = sem("proj_ready")
        ss_ready = sem("ss_ready")
        pool_step = sem("pool_step")
        by_sin_ready = sem("by_sin_ready")
        rinv_ready = sem("rinv_ready")
        by_cos_ready = sem("by_cos_ready")
        rotated_ready = sem("rotated_ready")
        normed_ready = sem("normed_ready")
        turned = sem("turned")
        rot_copied = sem("rot_copied")
        stored = [sem("stored0"), sem("stored1")]

        PAIR = 2 * TILES
        V_UNITS = V_CHUNKS * TILES
        K_UNITS = K_CHUNKS * TILES
        PAIRS = (V_CHUNKS + K_CHUNKS + Q_CHUNKS) // 2
        N_ROT = (PAIRS - 1) * PAIR
        LAG = 2
        block = ctx.enter_context(nc.Block())

        def over_pairs(eng, body):
            for pair in range(3):
                body(pair, pair)
            with eng.Fori(3, PAIRS) as pair:
                body(pair, 3)

        def rot_kind(pair_kind, n):
            kind = pair_kind + (n // PAIR)
            return None if kind < 1 else "k" if kind == 1 else "q"

        @block.sync
        def _(sp):
            def load_w(chunk, par):
                wait(sp, w_lo_ready, KT * (chunk - 1))
                sp.dma_start(wraw[:, par, :, :], a["w_all"][chunk] if isinstance(chunk, int)
                             else a["w_all"][bass.ds(chunk, 1), :, :, :].rearrange("a p k n -> p (a k) n"))\
                  .then_inc(w_loaded[par], 16)

            for piece in range(X_PIECES):
                wait(sp, x_lo_ready, piece - X_STAGES + 1)
                sp.dma_start(xstage[:, piece % X_STAGES, :, :], a["xT"][:, piece, :, :]).then_inc(x_loaded[piece % X_STAGES], 16)
                if piece == 0:
                    load_w(0, 0)
            load_w(1, 1)

            def store(pair, n, kind):
                r = PAIR * (pair - 1) + n
                par, t, c = n % 2, n % TILES, (n % PAIR) // TILES
                seqs = slice(BPT * t, BPT * t + BPT)
                head = c * HPC if kind == "k" else (2 * (pair - 2) + n // TILES) * HPC
                if not isinstance(head, int):
                    head = sp.snap(head)
                wait(sp, rot_copied, r + 1)
                dst = scratch[kind][seqs, :, bass.ds(head, HPC), :]
                sp.dma_start(dst.rearrange("b d h s -> d b (h s)"),
                             rot_out[:, par, :, :, :].rearrange("d b h s -> d b (h s)")).then_inc(stored[par], 16)

            def body(pair, kind):
                for n in range(PAIR):
                    t, c = n % TILES, n // TILES
                    if t == 0 and kind * 2 + c >= 1:
                        chunk = 2 * pair + c + 1
                        if not isinstance(pair, int):
                            chunk = sp.snap(chunk)
                        load_w(chunk, (c + 1) % 2)
                    if kind == 0:
                        wait(sp, v_copied, n + 1)
                        sp.dma_start(scratch["v"][P * t:P * t + P, CH * c:CH * c + CH], vout[:, n % 2, :])\
                          .then_inc(v_stored[n % 2], 16)
                    m = n - LAG
                    if rot_kind(kind, m):
                        store(pair, m, rot_kind(kind, m))

            over_pairs(sp, body)
            for m in range(-LAG, 0):
                store(PAIRS, m, "q")
            for par in range(2):
                sp.wait_ge(v_stored[par], 16 * V_UNITS // 2)
                sp.wait_ge(stored[par], 16 * N_ROT // 2)
            sp.wait_ge(w_loaded[0], 16 * (PAIRS + 1))

        @block.gpsimd
        def _(pool):
            pool.dma_start(pos_i[:, :], a["seqlen_by_tile"]).then_inc(consts_loaded, 16)
            pool.dma_start(row_in_seq[:, :], a["row_in_seq"]).then_inc(consts_loaded, 16)
            pool.dma_start(inv_freq[:, :], a["inv_freq"]).then_inc(consts_loaded, 16)
            pool.dma_start(norm_w[:, 0, :], a["k_norm"]).then_inc(consts_loaded, 16)
            pool.dma_start(norm_w[:, 1, :], a["q_norm"]).then_inc(consts_loaded, 16)
            build_identity(pool, ident, ident_ready)
            pool.memset(minus_half[:, :], -0.5).then_inc(pool_step, 1)

            def body(pair, kind):
                if kind == 0:
                    return
                side = 0 if kind == 1 else 1
                for n in range(PAIR):
                    r, par, t = PAIR * (pair - 1) + n, n % 2, n % TILES
                    wait(pool, proj_ready, r + 1)
                    wait(pool, rotated_ready, r - 1)
                    if kind == 1 and n == 0:
                        pool.wait_ge(table_step, TABLE_STEPS)
                    swapped = proj[:, par, :, :].rearrange("p h (a c) -> p h a c", a=2)[:, :, ::-1, :]
                    pool.tensor_tensor(by_sin[:, par, :, :].rearrange("p h (a c) -> p h a c", a=2), swapped,
                                       sin_w[:, side, t:t + 1, :].rearrange("p o (a c) -> p o a c", a=2)
                                       .to_broadcast([P, HPC, 2, D // 2]), ALU.mult).then_inc(by_sin_ready, 1)
                    pool.wait_ge(table_step, TABLE_STEPS)
                    pool.wait_ge(ss_ready, r + 1)
                    pool.tensor_scalar(mean_sq[:, par, :], ss[:, par, :], 1.0 / D, EPS, ALU.mult, ALU.add)\
                        .then_inc(pool_step, 1)
                    pool.wait_ge(pool_step, r + 2)
                    wait(pool, normed_ready, r - 1)
                    pool.tensor_tensor(rinv[:, par, :], mean_sq[:, par, :], minus_half[:, :], ALU.pow)\
                        .then_inc(rinv_ready, 1)

            over_pairs(pool, body)

        @block.scalar
        def _(act):
            def split_next(pair, n):
                t, c = n % TILES, n // TILES
                if t % 3 == 0 and 3 <= t <= 12:
                    kt, par = t // 3 - 1, (c + 1) % 2
                    act.wait_ge(w_loaded[par], 16 * (pair + 1 + c))
                    wait(act, mm_done, PAIR * pair + TILES * c)
                    act.copy(wh[:, par, kt, :], wraw[:, par, kt, :]).then_inc(w_hi_ready, 1)

            for piece in range(X_PIECES):
                act.wait_ge(x_loaded[piece % X_STAGES], 16 * (piece // X_STAGES + 1))
                act.copy(xh[:, piece, :, :], xstage[:, piece % X_STAGES, :, :]).then_inc(x_hi_ready, 1)
                if piece == 0:
                    act.wait_ge(w_loaded[0], 16)
                    for kt in range(KT):
                        act.copy(wh[:, 0, kt, :], wraw[:, 0, kt, :]).then_inc(w_hi_ready, 1)

            def sines():
                act.wait_ge(table_step, ANGLE_STEPS)
                act.activation(sine[:, :, :], angle[:, :, :], ACT.Sin).then_inc(sines_ready, 1)
                act.activation(cosine, angle[:, :, :], ACT.Sin, scale=0.5).then_inc(sines_ready, 1)

            def turned_out(pair, n):
                r, par = PAIR * (pair - 1) + n, n % 2
                src = ps[:, 4 + par, :].rearrange("d (h b s) -> d b h s", h=HPC, b=BPT)
                act.wait_ge(turned, r + 1)
                wait(act, stored[par], 16 * (PAIR // 2 * (pair - 1) + n // 2))
                act.copy(rot_out[:, par, :, :, :], src).then_inc(rot_copied, 1)

            def body(pair, kind):
                for n in range(PAIR):
                    g, par = PAIR * pair + n, n % 2
                    if kind == 0:
                        act.wait_ge(mm_done, g + 1)
                        wait(act, v_stored[par], 16 * (n // 2))
                        act.copy(vout[:, par, :], ps[:, n % 4, :]).then_inc(v_copied, 1)
                        if n == TILES - 2:
                            sines()
                    else:
                        r = PAIR * (pair - 1) + n
                        act.wait_ge(mm_done, g + 1)
                        wait(act, rotated_ready, r - 1)
                        act.copy(proj[:, par, :, :], ps[:, n % 4, :].rearrange("p (h d) -> p h d", h=HPC))\
                           .then_inc(proj_ready, 1)
                        wait(act, ss_ready, r - 1)
                        wait(act, rinv_ready, r - 1)
                        for h in range(HPC):
                            last = act.activation(square[:, par, h, :], ps[:, n % 4, D * h:D * h + D], ACT.Square,
                                                  accum_out=ss[:, par, h:h + 1])
                        last.then_inc(ss_ready, 1)
                    m = n - LAG
                    if rot_kind(kind, m):
                        turned_out(pair, m)
                    split_next(pair, n)

            over_pairs(act, body)
            for m in range(-LAG, 0):
                turned_out(PAIRS, m)

        @block.vector
        def _(dve):
            def split_next(pair, n):
                t, c = n % TILES, n // TILES
                if t % 3 == 0 and 3 <= t <= 12:
                    kt, par = t // 3 - 1, (c + 1) % 2
                    dve.wait_ge(w_hi_ready, KT * (2 * pair + c + 1) + kt + 1)
                    dve.tensor_tensor(wl[:, par, kt, :], wraw[:, par, kt, :], wh[:, par, kt, :].bitcast(F32),
                                      ALU.subtract).then_inc(w_lo_ready, 1)

            for piece in range(X_PIECES):
                dve.wait_ge(x_hi_ready, piece + 1)
                dve.tensor_tensor(xl[:, piece, :, :], xstage[:, piece % X_STAGES, :, :], xh[:, piece, :, :].bitcast(F32),
                                  ALU.subtract).then_inc(x_lo_ready, 1)
                if piece == 0:
                    for kt in range(KT):
                        dve.wait_ge(w_hi_ready, kt + 1)
                        dve.tensor_tensor(wl[:, 0, kt, :], wraw[:, 0, kt, :], wh[:, 0, kt, :].bitcast(F32),
                                          ALU.subtract).then_inc(w_lo_ready, 1)

            done = 0

            def step(instruction):
                nonlocal done
                instruction.then_inc(table_step, 1)
                done += 1
                dve.wait_ge(table_step, done)

            dve.wait_ge(consts_loaded, 80)
            step(dve.tensor_copy(pos[:, :], pos_i[:, :]))
            step(dve.tensor_tensor(pos[:, :], pos[:, :], row_in_seq[:, :].to_broadcast([P, TILES]), ALU.add))
            step(dve.tensor_tensor(angle[:, :, :], pos[:, :].unsqueeze(2).to_broadcast([P, TILES, D // 2]),
                                   inv_freq[:, :].unsqueeze(1).to_broadcast([P, TILES, D // 2]), ALU.mult))
            step(dve.tensor_scalar(turns[:, :, :], angle[:, :, :], float(1 / (2 * np.pi)), None, ALU.mult))
            step(dve.tensor_copy(sine[:, :, :], turns[:, :, :]))
            step(dve.scalar_tensor_tensor(out=angle[:, :, :], in0=sine[:, :, :], scalar=-TWO_PI_1,
                                          in1=angle[:, :, :], op0=ALU.mult, op1=ALU.add))
            step(dve.scalar_tensor_tensor(out=angle[:, :, :], in0=sine[:, :, :], scalar=-TWO_PI_2,
                                          in1=angle[:, :, :], op0=ALU.mult, op1=ALU.add))
            step(dve.scalar_tensor_tensor(out=angle[:, :, :], in0=sine[:, :, :], scalar=-TWO_PI_3,
                                          in1=angle[:, :, :], op0=ALU.mult, op1=ALU.add))
            step(dve.tensor_scalar(angle[:, :, :], angle[:, :, :], PI_BELOW, -PI_BELOW, ALU.min, ALU.max))
            assert done == ANGLE_STEPS, done
            for n in range(TILES):
                split_next(0, n)
            dve.wait_ge(sines_ready, 2)
            step(dve.tensor_tensor(cosine, cosine, cosine, ALU.mult))
            step(dve.tensor_scalar(cosine, cosine, -2.0, 1.0, ALU.mult, ALU.add))
            step(dve.tensor_scalar(norm_w[:, 1, :], norm_w[:, 1, :], -SCALE, None, ALU.mult))
            half = D // 2
            for side in range(2):
                for lo, hi in ((0, half), (half, D)):
                    w_here = norm_w[:, side, lo:hi].unsqueeze(1).to_broadcast([P, TILES, half])
                    step(dve.tensor_tensor(cos_w[:, side, :, lo:hi], cosine, w_here, ALU.mult))
                first = norm_w[:, side, 0:half].unsqueeze(1).to_broadcast([P, TILES, half])
                second = norm_w[:, side, half:D].unsqueeze(1).to_broadcast([P, TILES, half])
                step(dve.tensor_tensor(sin_w[:, side, :, half:D], sine[:, :, :], first, ALU.mult))
                step(dve.scalar_tensor_tensor(out=sin_w[:, side, :, 0:half], in0=sine[:, :, :], scalar=-1.0,
                                              in1=second, op0=ALU.mult, op1=ALU.mult))
            assert done == TABLE_STEPS, done

            def body(pair, kind):
                for n in range(0 if kind else TILES, PAIR):
                    if kind:
                        r, par, t = PAIR * (pair - 1) + n, n % 2, n % TILES
                        side = 0 if kind == 1 else 1
                        dve.wait_ge(proj_ready, r + 1)
                        dve.tensor_tensor(by_cos[:, :, :], proj[:, par, :, :],
                                          cos_w[:, side, t:t + 1, :].to_broadcast([P, HPC, D]), ALU.mult)\
                           .then_inc(by_cos_ready, 1)
                        dve.wait_ge(by_cos_ready, r + 1)
                        dve.wait_ge(by_sin_ready, r + 1)
                        dve.tensor_tensor(rotated[:, :, :], by_cos[:, :, :], by_sin[:, par, :, :], ALU.add)\
                           .then_inc(rotated_ready, 1)
                        dve.wait_ge(rotated_ready, r + 1)
                        dve.wait_ge(rinv_ready, r + 1)
                        wait(dve, turned, r - 1)
                        dve.tensor_tensor(normed[:, par, :, :], rotated[:, :, :],
                                          rinv[:, par, :].unsqueeze(2).to_broadcast([P, HPC, D]), ALU.mult)\
                           .then_inc(normed_ready, 1)
                    split_next(pair, n)

            over_pairs(dve, body)

        @block.tensor
        def _(pe):
            pe.wait_ge(ident_ready, 2)

            def turn(pair, n):
                r, par = PAIR * (pair - 1) + n, n % 2
                pe.wait_ge(normed_ready, r + 1)
                wait(pe, rot_copied, r - 1)
                for h in range(HPC):
                    last = pe.transpose(ps[:, 4 + par, P * h:P * h + P], normed[:, par, h, :], ident[:, :])
                last.then_inc(turned, 1)

            def body(pair, kind):
                for n in range(PAIR):
                    g, t, c = PAIR * pair + n, n % TILES, n // TILES
                    if t == 0 and kind + c > 0:
                        pe.wait_ge(w_lo_ready, KT * (2 * pair + c + 1))
                    if kind == 0 and c == 0 and t % X_TILES == 0:
                        pe.wait_ge(x_lo_ready, t // X_TILES + 1)
                    if kind == 0 or (kind == 1 and n < 4):
                        wait(pe, v_copied, g - 3)
                    else:
                        wait(pe, ss_ready, g - V_UNITS - 3)
                    cols = slice(P * (t % X_TILES), P * (t % X_TILES) + P)
                    for kt in range(KT):
                        if kind == 0 and n == 0:
                            pe.wait_ge(w_lo_ready, kt + 1)
                        for x_part, w_part in ((xh, wh), (xl, wh), (xh, wl)):
                            last = pe.matmul(ps[:, n % 4, :], x_part[:, t // X_TILES, kt, cols], w_part[:, c, kt, :],
                                             start=(kt == 0 and x_part is xh and w_part is wh),
                                             stop=(kt == KT - 1 and w_part is wl))
                    last.then_inc(mm_done, 1)
                    m = n - LAG
                    if rot_kind(kind, m):
                        turn(pair, m)

            over_pairs(pe, body)
            for m in range(-LAG, 0):
                turn(PAIRS, m)


def attend(nc, ps, a, scratch):
    with ExitStack() as ctx:
        def sb(name, shape, dt=F32):
            return ctx.enter_context(nc.sbuf_tensor("a_" + name, shape, dt))

        def sem(name):
            return ctx.enter_context(nc.semaphore("a_" + name))

        RING = 4
        KEY_TILES = CACHED // P + 1
        BLOCKS = NPP + 1 + REP
        HALF_HEADS = HK // 2
        HALF = HALF_HEADS * D
        GATHERS = KEY_TILES - 1
        HALVES = HK // HALF_HEADS
        SLOTS = 4
        HALF_KEYS = KEYS // 2
        SETUP_STEPS = 2
        OUT_BANK = 6

        def turn_bank(n, new=False):
            return 4 + (n + n // HALF_HEADS + new) % 2

        CACHE_PARTS = 8
        kcache = sb("kcache", [P, PAGES, HK, PSIZE])
        kqraw = sb("kqraw", [P, 2, BLOCKS, HK, PSIZE])
        kqhi = sb("kqhi", [P, RING, KEYS + P], F32R)
        kqlo = sb("kqlo", [P, RING, KEYS + P], F32R)
        v = sb("v", [P, 2, KEY_TILES, HK * D])
        v_new = sb("v_new", [P, 2, HALVES, D])
        key_pos = sb("key_pos", [P, KEYS])
        mask = sb("mask", [P, 2, KEYS])
        seqlen_i = sb("seqlen_i", [P, BATCH], I32)
        seqlen = sb("seqlen", [P, BATCH])
        page_of_row = sb("page_of_row", [P, BATCH * GATHERS], I32)
        row_in_page = sb("row_in_page", [P, 1])
        vrow = sb("vrow", [P, BATCH * GATHERS], I32)
        vrow_now = sb("vrow_now", [P, 2, GATHERS], I32)
        scores = sb("scores", [P, 2, KEYS])
        nmax = sb("nmax", [P, 2])
        probs = sb("probs", [P, SLOTS, KEYS])
        probs_new = sb("probs_new", [P, 2, HALF_HEADS, SEQ])
        sums = sb("sums", [P, 4])
        rsum = sb("rsum", [P, 4])
        probsT = sb("probsT", [P, 2, GATHERS, P])
        probsT_new = sb("probsT_new", [P, 2, P])
        oT = sb("oT", [P, HALVES, HALF_HEADS * REP * SEQ])
        ident = sb("ident", [P, P])

        consts_loaded = sem("consts_loaded")
        kcache_loaded = sem("kcache_loaded")
        kq_loaded = [sem("kq_loaded0"), sem("kq_loaded1")]
        v_loaded = [sem("v_loaded0"), sem("v_loaded1")]
        v_new_loaded = [sem("v_new_loaded0"), sem("v_new_loaded1")]
        v_new_placed = sem("v_new_placed")
        o_stored = [sem("o_stored0"), sem("o_stored1")]
        pool_passed = sem("pool_passed")
        dve_passed = sem("dve_passed")
        ident_ready = sem("ident_ready")
        key_pos_ready = sem("key_pos_ready")
        zeroed = sem("zeroed")
        setup_done = sem("setup_done")
        vrow_now_ready = sem("vrow_now_ready")
        mask_ready = sem("mask_ready")
        kq_hi_ready = sem("kq_hi_ready")
        kq_lo_ready = sem("kq_lo_ready")
        qk_done = sem("qk_done")
        scores_masked = sem("scores_masked")
        probs_ready = sem("probs_ready")
        probs_turned = sem("probs_turned")
        probsT_ready = sem("probsT_ready")
        new_turned = sem("new_turned")
        probsT_new_ready = sem("probsT_new_ready")
        pv_done = sem("pv_done")
        group_done = sem("group_done")
        rsum_ready = sem("rsum_ready")
        probs_scaled = sem("probs_scaled")
        new_scaled = sem("new_scaled")
        oT_ready = sem("oT_ready")

        PAIR = 2 * HK
        UNITS = BATCH * HK
        block = ctx.enter_context(nc.Block())

        def over_units(eng, step, lag):
            for n in range(PAIR):
                step(0, n)
            with eng.Fori(1, BATCH // 2) as i:
                for n in range(PAIR):
                    step(i, n)
            for n in range(lag):
                step(BATCH // 2, n)

        def there(i, n, total=UNITS):
            return not isinstance(i, int) or 0 <= PAIR * i + n < total

        @block.sync
        def _(sp):
            page = [sp.alloc_register(f"page{j}") for j in range(NPP)]

            def load_keys(b, par, source):
                sp.load(page, a["block_table"][bass.ds(b, 1), :])
                wait(sp, kq_lo_ready, HK * (b - 1))
                for j in range(NPP):
                    at = sp.snap(page[j], min_val=0, max_val=PAGES - 1)
                    sp.dma_start(kqraw[:, par, j, :, :], source[:, bass.ds(at, 1), :, :])\
                      .then_inc(kq_loaded[par], 16)
                sp.dma_start(kqraw[:, par, NPP, :, :], scratch["k"][bass.ds(b, 1), :, :, :]
                             .rearrange("o d h s -> d (o h) s")).then_inc(kq_loaded[par], 16)
                sp.dma_start(kqraw[:, par, NPP + 1:BLOCKS, :, :].rearrange("d g h s -> d (g h s)"),
                             scratch["q"][bass.ds(b, 1), :, :, :].rearrange("o d h s -> d (o h s)"))\
                  .then_inc(kq_loaded[par], 16)

            def load_new_v(b, par):
                wait(sp, v_new_placed, HK * (b - 1))
                for half in range(HALVES):
                    src = scratch["v"][bass.ds(SEQ * b, SEQ), HALF * half:HALF * half + HALF]
                    sp.dma_start(v_new[:, par, half, :], src.rearrange("s (h d) -> h s d", h=HALF_HEADS))\
                      .then_inc(v_new_loaded[par], 16)

            def store(b):
                for half in range(HALVES):
                    heads = slice(HALF_HEADS * REP * half, HALF_HEADS * REP * (half + 1))
                    sp.wait_ge(oT_ready, HALVES * b + half + 1)
                    sp.dma_start(scratch["o"][bass.ds(b, 1), :, heads, :].rearrange("o d h s -> d (o h s)"),
                                 oT[:, half, :]).then_inc(o_stored[half], 16)

            def sequence(b, par, source):
                if not (isinstance(b, int) and b in (0, BATCH - 1)):
                    load_new_v(b + 1, 1 - par)
                    load_keys(b + 1, 1 - par, source)
                if not (isinstance(b, int) and b == 0):
                    store(b - 1)

            def load_cache(parts):
                for part in parts:
                    pages = slice(PAGES // CACHE_PARTS * part, PAGES // CACHE_PARTS * (part + 1))
                    sp.dma_start(kcache[:, pages, :, :], a["k_cacheT"][:, pages, :, :]).then_inc(kcache_loaded, 16)

            for b in range(2):
                load_keys(b, b, a["k_cacheT"])
                load_new_v(b, b)
            sequence(0, 0, a["k_cacheT"])
            sequence(1, 1, a["k_cacheT"])
            load_cache(range(2))
            sequence(2, 0, a["k_cacheT"])
            load_cache(range(2, 5))
            sequence(3, 1, a["k_cacheT"])
            load_cache(range(5, CACHE_PARTS))
            sp.wait_ge(kcache_loaded, 16 * CACHE_PARTS)
            with sp.Fori(2, BATCH // 2 - 1) as i:
                for par in range(2):
                    sequence(sp.snap(2 * i + par), par, kcache)
            sequence(BATCH - 2, 0, kcache)
            sequence(BATCH - 1, 1, kcache)
            store(BATCH - 1)
            for half in range(HALVES):
                sp.wait_ge(o_stored[half], 16 * BATCH)

        @block.gpsimd
        def _(pool):
            pool.dma_start(seqlen_i[:, :], a["seqlen_all"]).then_inc(consts_loaded, 16)
            pool.dma_start(page_of_row[:, :], a["page_of_row"]).then_inc(consts_loaded, 16)
            pool.dma_start(row_in_page[:, :], a["row_in_page"]).then_inc(consts_loaded, 16)
            build_identity(pool, ident, ident_ready)
            pool.iota(key_pos[:, 0:CACHED], pattern=[[1, CACHED]], base=0, channel_multiplier=0,
                      allow_small_or_imprecise_dtypes=True).then_inc(key_pos_ready, 1)
            pool.memset(key_pos[:, CACHED:KEYS], -1.0).then_inc(key_pos_ready, 1)
            pool.wait_ge(setup_done, SETUP_STEPS)

            def gather(i, par):
                b = 2 * i + par
                if not isinstance(b, int):
                    b = pool.snap(b)
                wait(pool, v_loaded[1 - par], 16 * GATHERS * (i + par))
                pool.tensor_copy(vrow_now[:, par, :], vrow[:, bass.ds(GATHERS * b, GATHERS)])\
                    .then_inc(vrow_now_ready, 1)
                wait_all(pool, pool_passed, (vrow_now_ready, b + 1), (group_done, HALVES * (b - 1)),
                         (v_new_loaded[par], 16 * HALVES * (i + 1)))
                for h in range(HK):
                    at = h % HALF_HEADS
                    rows, cols = slice(SEQ * at, SEQ * at + SEQ), slice(D * h, D * h + D)
                    pool.tensor_copy(v[rows, par, GATHERS, cols], v_new[rows, par, h // HALF_HEADS, :])\
                        .then_inc(v_new_placed, 1)
                wait_all(pool, pool_passed, (v_new_placed, HK * (b + 1)))
                for j in range(GATHERS):
                    pool.indirect_dma_start(
                        v[:, par, j, :], None, a["v_rows"],
                        bass.IndirectOffsetOnAxis(ap=vrow_now[:, par, j:j + 1], axis=0))\
                        .then_inc(v_loaded[par], 16)

            gather(0, 0)
            gather(0, 1)
            with pool.Fori(1, BATCH // 2) as i:
                for par in range(2):
                    gather(i, par)

        @block.scalar
        def _(act):
            def split_high(i, n):
                u, par = PAIR * i + n, n // HK
                if n % HK == 0:
                    act.wait_ge(kq_loaded[par], 16 * (NPP + 2) * (i + 1))
                wait(act, qk_done, u - RING + 1)
                act.copy(kqhi[:, n % RING, :].rearrange("d (j s) -> d j s", s=PSIZE), kqraw[:, par, :, n % HK, :])\
                   .then_inc(kq_hi_ready, 1)

            def exponentials(i, n):
                u, par = PAIR * i + n, n % 2
                act.wait_ge(scores_masked, u + 1)
                wait(act, probs_turned, u - SLOTS + 1)
                wait(act, new_scaled, u - SLOTS + 1)
                wait(act, rsum_ready, u - 3)
                act.activation(probs[:, n % SLOTS, :], scores[:, par, :], ACT.Exp, bias=nmax[:, par:par + 1],
                               scale=-1.0, accum_out=sums[:, n % 4:n % 4 + 1]).then_inc(probs_ready, 1)

            def turned_out(i, n):
                u, par = PAIR * i + n, n % 2
                act.wait_ge(probs_turned, u + 1)
                wait(act, pv_done, u - 1)
                act.copy(probsT[:, par, :, :].rearrange("k j q -> k (j q)"), ps[:, turn_bank(n), :])\
                   .then_inc(probsT_ready, 1)
                if n % HALF_HEADS == HALF_HEADS - 1:
                    group, g_par = (PAIR // HALF_HEADS) * i + n // HALF_HEADS, (n // HALF_HEADS) % 2
                    act.wait_ge(new_turned, group + 1)
                    wait(act, group_done, group - 1)
                    act.copy(probsT_new[:, g_par, :], ps[:, turn_bank(n, True), 0:P]).then_inc(probsT_new_ready, 1)

            def group_out(i, n):
                group, half = (PAIR // HALF_HEADS) * i + n // HALF_HEADS, (n // HALF_HEADS) % HALVES
                wait(act, o_stored[half], 16 * (2 * i + n // HK))
                act.wait_ge(group_done, group + 1)
                act.copy(oT[:, half, :], ps[:, OUT_BANK + half, :]).then_inc(oT_ready, 1)

            def step(i, n):
                if there(i, n - 5):
                    turned_out(i, n - 5)
                if there(i, n - 6) and (n - 6) % HALF_HEADS == HALF_HEADS - 1:
                    group_out(i, n - 6)
                if there(i, n - 3):
                    exponentials(i, n - 3)
                if there(i, n):
                    split_high(i, n)

            over_units(act, step, 6)

        @block.vector
        def _(dve):
            dve.memset(v[:, :, GATHERS, :], 0.0).then_inc(zeroed, 1)
            dve.wait_ge(consts_loaded, 48)
            dve.tensor_copy(seqlen[:, :], seqlen_i[:, :]).then_inc(setup_done, 1)
            dve.tensor_scalar(vrow[:, :], page_of_row[:, :], float(PSIZE), row_in_page[:, 0:1],
                              ALU.mult, ALU.add).then_inc(setup_done, 1)
            dve.wait_ge(setup_done, SETUP_STEPS)
            dve.wait_ge(key_pos_ready, 2)

            def make_mask(i, n):
                b, par = 2 * i + n // HK, n // HK
                dve.tensor_scalar(mask[:, par, :], key_pos[:, :], seqlen[:, bass.ds(b, 1)], MASKED,
                                  ALU.is_ge, ALU.mult).then_inc(mask_ready, 1)

            def split_low(i, n):
                u, par = PAIR * i + n, (n // HK) % 2
                dve.wait_ge(kq_hi_ready, u + 1)
                dve.tensor_tensor(kqlo[:, n % RING, :].rearrange("d (j s) -> d j s", s=PSIZE),
                                  kqraw[:, par, :, n % HK, :],
                                  kqhi[:, n % RING, :].bitcast(F32).rearrange("d (j s) -> d j s", s=PSIZE),
                                  ALU.subtract).then_inc(kq_lo_ready, 1)

            def mask_scores(i, n):
                u, par = PAIR * i + n, n % 2
                wait_all(dve, dve_passed, (qk_done, u + 1), (mask_ready, 2 * i + n // HK + 1),
                         (probs_ready, u - 1))
                dve.tensor_tensor_reduce(scores[:, par, :].rearrange("q (a k) -> q a k", a=2),
                                         ps[:, 2 * par:2 * par + 2, 0:HALF_KEYS],
                                         mask[:, (n // HK) % 2, :].rearrange("q (a k) -> q a k", a=2),
                                         1.0, 0.0 + 3e38, ALU.add, ALU.min, nmax[:, par:par + 1])\
                   .then_inc(scores_masked, 1)

            def invert_sum(i, n):
                u = PAIR * i + n
                dve.wait_ge(probs_ready, u + 1)
                dve.reciprocal(rsum[:, n % 4:n % 4 + 1], sums[:, n % 4:n % 4 + 1]).then_inc(rsum_ready, 1)

            def scale(i, n):
                u = PAIR * i + n
                dve.wait_ge(rsum_ready, u + 1)
                dve.tensor_scalar(probs[:, n % SLOTS, 0:CACHED], probs[:, n % SLOTS, 0:CACHED],
                                  rsum[:, n % 4:n % 4 + 1], None, ALU.mult).then_inc(probs_scaled, 1)
                group, place = (PAIR // HALF_HEADS) * i + n // HALF_HEADS, n % HALF_HEADS
                if place == 0:
                    wait(dve, new_turned, group - 1)
                dve.tensor_scalar(probs_new[:, (n // HALF_HEADS) % 2, place, :], probs[:, n % SLOTS, CACHED:KEYS],
                                  rsum[:, n % 4:n % 4 + 1], None, ALU.mult).then_inc(new_scaled, 1)

            def step(i, n):
                if there(i, n) and n % HK == 0:
                    make_mask(i, n)
                if there(i, n - 4):
                    invert_sum(i, n - 4)
                if there(i, n - 3):
                    mask_scores(i, n - 3)
                if there(i, n - 4):
                    scale(i, n - 4)
                if there(i, n - 1):
                    split_low(i, n - 1)

            over_units(dve, step, 4)

        @block.tensor
        def _(pe):
            pe.wait_ge(ident_ready, 2)

            def score(i, n):
                u, par = PAIR * i + n, n % 2
                pe.wait_ge(kq_lo_ready, u + 1)
                wait(pe, scores_masked, u - 1)
                slot, q_cols = n % RING, slice(KEYS, KEYS + P)
                for part in range(2):
                    keys = slice(HALF_KEYS * part, HALF_KEYS * part + HALF_KEYS)
                    out = ps[:, 2 * par + part, 0:HALF_KEYS]
                    pe.matmul(out, kqhi[:, slot, q_cols], kqhi[:, slot, keys], start=True, stop=False)
                    pe.matmul(out, kqhi[:, slot, q_cols], kqlo[:, slot, keys], start=False, stop=False)
                    last = pe.matmul(out, kqlo[:, slot, q_cols], kqhi[:, slot, keys], start=False, stop=True)
                last.then_inc(qk_done, 1)

            def turn_probs(i, n):
                u, par = PAIR * i + n, n % 2
                pe.wait_ge(probs_scaled, u + 1)
                group, place = (PAIR // HALF_HEADS) * i + n // HALF_HEADS, n % HALF_HEADS
                if place == 1:
                    wait(pe, probsT_new_ready, group)
                else:
                    wait(pe, probsT_ready, u if place == 0 else u - 1)
                for j in range(GATHERS):
                    last = pe.transpose(ps[:, turn_bank(n), P * j:P * j + P], probs[:, n % SLOTS, P * j:P * j + P],
                                        ident[:, :])
                last.then_inc(probs_turned, 1)
                if place == HALF_HEADS - 1:
                    pe.wait_ge(new_scaled, u + 1)
                    wait(pe, probsT_ready, u)
                    pe.transpose(ps[:, turn_bank(n, True), 0:P], probs_new[:, (n // HALF_HEADS) % 2, :, :]
                                 .rearrange("q h s -> q (h s)"), ident[:, :]).then_inc(new_turned, 1)

            def weigh(i, n):
                u, par, b_par, half = PAIR * i + n, n % 2, (n // HK) % 2, (n % HK) // HALF_HEADS
                group, place = (PAIR // HALF_HEADS) * i + n // HALF_HEADS, n % HALF_HEADS
                if n % HK == 0:
                    pe.wait_ge(v_loaded[b_par], 16 * GATHERS * (i + n // PAIR + 1))
                    pe.wait_ge(v_new_placed, HK * (2 * i + n // HK + 1))
                if place == 0:
                    wait(pe, oT_ready, group - 1)
                pe.wait_ge(probsT_ready, u + 1)
                for j in range(GATHERS):
                    last = pe.matmul(ps[:, OUT_BANK + half, P * place:P * place + P],
                                     v[:, b_par, j, D * (n % HK):D * (n % HK) + D], probsT[:, par, j, :],
                                     start=(place == 0 and j == 0), stop=False)
                last.then_inc(pv_done, 1)
                if place == HALF_HEADS - 1:
                    pe.wait_ge(probsT_new_ready, group + 1)
                    for h in range(HALF_HEADS):
                        cols = slice(HALF * half + D * h, HALF * half + D * h + D)
                        last = pe.matmul(ps[:, OUT_BANK + half, P * h:P * h + P], v[:, b_par, GATHERS, cols],
                                         probsT_new[:, half, :],
                                         start=False, stop=(h == HALF_HEADS - 1))
                    last.then_inc(group_done, 1)

            def step(i, n):
                if there(i, n):
                    score(i, n)
                if there(i, n - 2):
                    turn_probs(i, n - 2)
                if there(i, n - 3):
                    weigh(i, n - 3)

            over_units(pe, step, 3)


def finish(nc, ps, a, scratch, out):
    with ExitStack() as ctx:
        def sb(name, shape, dt=F32):
            return ctx.enter_context(nc.sbuf_tensor("f_" + name, shape, dt))

        def sem(name):
            return ctx.enter_context(nc.semaphore("f_" + name))

        QUARTER = HQ // 8
        CHUNKS = HQ // QUARTER
        G = BPT * RANK
        STAGES = 4
        stage = sb("stage", [P, STAGES, HID])
        woh = sb("woh", [P, HQ, HID], F32R)
        wol = sb("wol", [P, HQ, HID], F32R)
        bwh = sb("bwh", [P, 2, KT, HID], F32R)
        bwl = sb("bwl", [P, 2, KT, HID], F32R)
        o_raw = sb("o_raw", [P, 2, BPT, QUARTER, SEQ])
        oh = sb("oh", [P, 2, QUARTER, P], F32R)
        ol = sb("ol", [P, 2, QUARTER, P], F32R)
        x_in = sb("x_in", [P, HID])
        x_now = sb("x_now", [P, 2, HID])
        xT = sb("xT", [P, KT, P])
        xTh = sb("xTh", [P, KT, P], F32R)
        xTl = sb("xTl", [P, KT, P], F32R)
        down = sb("down", [G, 3, HID])
        downT = sb("downT", [P, KT, G])
        up = sb("up", [P, 3, HID])
        hidden = sb("hidden", [P, P])
        own = sb("own", [G, P])
        ident = sb("ident", [P, P])
        adapter = sb("adapter", [G, 3, TILES], I32)
        rank_row = sb("rank_row", [G, 1])
        row = sb("row", [G, 3, TILES], I32)
        row_now = sb("row_now", [G, 2, 3], I32)

        consts_loaded = sem("consts_loaded")
        stage_loaded = [sem(f"stage_loaded{i}") for i in range(STAGES)]
        w_hi_ready = sem("w_hi_ready")
        w_lo_ready = sem("w_lo_ready")
        bias_loaded = sem("bias_loaded")
        zeroed = sem("zeroed")
        pool_passed = sem("pool_passed")
        pe_passed = sem("pe_passed")
        ident_ready = sem("ident_ready")
        own_ready = sem("own_ready")
        row_ready = sem("row_ready")
        row_now_ready = sem("row_now_ready")
        adapters_loaded = [sem(f"adapters_loaded{layer}") for layer in range(3)]
        x_loaded = sem("x_loaded")
        o_loaded = [sem("o_loaded0"), sem("o_loaded1")]
        o_hi_ready = sem("o_hi_ready")
        o_lo_ready = sem("o_lo_ready")
        o_used = sem("o_used")
        x1_ready = sem("x1_ready")
        x_turned = sem("x_turned")
        down_turned = sem("down_turned")
        xT_ready = sem("xT_ready")
        xTh_ready = sem("xTh_ready")
        xTl_ready = sem("xTl_ready")
        downT_ready = sem("downT_ready")
        hidden_done = sem("hidden_done")
        hidden_ready = sem("hidden_ready")
        layer_done = sem("layer_done")
        x_ready = sem("x_ready")
        out_stored = sem("out_stored")

        PIECES = HQ + 2 * KT
        PIECES_PER_CHUNK = PIECES // CHUNKS

        def piece(p, high):
            if p < HQ:
                return (woh if high else wol)[:, p, :]
            return (bwh if high else bwl)[:, (p - HQ) // KT, p % KT, :]

        def pieces_of(t, c):
            return range(PIECES_PER_CHUNK * c, PIECES_PER_CHUNK * (c + 1)) if is_number(t, 0) else ()

        TURN_SLOT = {0: 0, 2: 1, 5: 2}
        HIDDEN_SLOT = {1: 0, 3: 1, 6: 2}
        END_SLOT = {1: 0, 4: 1, 6: 2}
        HAS_BASE = {0: 0, 2: 1}
        block = ctx.enter_context(nc.Block())

        def over_tiles(eng, tile):
            tile(0, 0)
            tile(1, 1)
            with eng.Fori(1, TILES // 2 - 1) as i:
                for par in range(2):
                    tile(eng.snap(2 * i + par), par)
            tile(TILES - 2, 0)
            tile(TILES - 1, 1)

        def is_number(t, number):
            return isinstance(t, int) and t == number

        def o_chunk(t, c):
            return scratch["o"][bass.ds(BPT * t, BPT), :, QUARTER * c:QUARTER * c + QUARTER, :]\
                .rearrange("b d h s -> d b (h s)")

        def as_loaded(buffer, par):
            return buffer[:, par, :, :, :].rearrange("d b h s -> d b (h s)")

        @block.sync
        def _(sp):
            for c in range(2):
                sp.dma_start(as_loaded(o_raw, c), o_chunk(0, c)).then_inc(o_loaded[c], 16)

            def tile(t, par):
                for c in range(CHUNKS):
                    for p in pieces_of(t, c):
                        wait(sp, w_lo_ready, p - STAGES + 1)
                        src = a["woT"][:, p, :] if p < HQ else a["baseT"][:, (p - HQ) // KT, p % KT, :]
                        sp.dma_start(stage[:, p % STAGES, :], src).then_inc(stage_loaded[p % STAGES], 16)
                    if not (is_number(t, TILES - 1) and c + 2 >= CHUNKS):
                        sp.wait_ge(o_lo_ready, CHUNKS * t + c + 1)
                        ahead = (t, c + 2) if c + 2 < CHUNKS else (t + 1, c + 2 - CHUNKS)
                        sp.dma_start(as_loaded(o_raw, c % 2), o_chunk(*ahead)).then_inc(o_loaded[c % 2], 16)
                    if c == 3:
                        wait(sp, x1_ready, t)
                        sp.dma_start(x_in[:, :], a["x"][bass.ds(P * t, P), :]).then_inc(x_loaded, 16)
                if is_number(t, 0):
                    sp.wait_ge(zeroed, 4)
                    for layer, name in ((0, "bias1"), (2, "bias3")):
                        sp.dma_start(up[G:G + 1, layer, :], a[name]).then_inc(bias_loaded, 16)
                else:
                    put(t - 1)

            def put(t):
                sp.wait_ge(x_ready, 3 * (t + 1))
                sp.dma_start(out[bass.ds(P * t, P), :], x_now[:, 1, :]).then_inc(out_stored, 16)

            over_tiles(sp, tile)
            put(TILES - 1)
            sp.wait_ge(out_stored, 16 * TILES)

        @block.gpsimd
        def _(pool):
            pool.dma_start(adapter[:, :, :], a["adapter_by_tile"]).then_inc(consts_loaded, 16)
            pool.dma_start(rank_row[:, :], a["rank_row"]).then_inc(consts_loaded, 16)
            pool.dma_start(own[:, :], a["own"]).then_inc(own_ready, 16)
            build_identity(pool, ident, ident_ready)
            pool.wait_ge(row_ready, 1)

            def gather(t, par):
                for layer in range(3):
                    wait(pool, adapters_loaded[layer], 32 * (t - 1))
                pool.tensor_copy(row_now[:, par, :], row[:, :, bass.ds(t, 1)].rearrange("g l o -> g (l o)"))\
                    .then_inc(row_now_ready, 1)
                wait_all(pool, pool_passed, (row_now_ready, t + 1))
                for layer in range(3):
                    wait_all(pool, pool_passed, (layer_done, 3 * (t - 1) + layer + 1))
                    for dst, name in ((down, "down"), (up, "up")):
                        pool.indirect_dma_start(
                            dst[0:G, layer, :], None, a[f"{name}{layer + 1}"],
                            bass.IndirectOffsetOnAxis(ap=row_now[:, par, layer:layer + 1], axis=0))\
                            .then_inc(adapters_loaded[layer], 16)

            over_tiles(pool, gather)

        @block.scalar
        def _(act):
            def split_high(t, c):
                n, par = CHUNKS * t + c, c % 2
                act.wait_ge(o_loaded[par], 16 * (CHUNKS // 2 * t + c // 2 + 1))
                wait(act, o_used, n - 1)
                act.copy(oh[:, par, :, :].rearrange("d h (b s) -> d h b s", b=BPT),
                         o_raw[:, par, :, :, :].rearrange("d b h s -> d h b s")).then_inc(o_hi_ready, 1)

            def chain(t, c):
                if c in TURN_SLOT:
                    k = 3 * t + TURN_SLOT[c]
                    turned = ps[:, 2, :].rearrange("i (k r) -> i k r", k=KT)
                    act.wait_ge(x_turned, k + 1)
                    wait(act, layer_done, k)
                    if TURN_SLOT[c] in HAS_BASE:
                        act.copy(xTh[:, :, :], turned).then_inc(xTh_ready, 1)
                    act.copy(xT[:, :, :], turned).then_inc(xT_ready, 1)
                    act.wait_ge(down_turned, k + 1)
                    act.copy(downT[:, :, :], ps[:, 3, 0:KT * G].rearrange("i (k g) -> i k g", k=KT))\
                       .then_inc(downT_ready, 1)

            def tile(t, par):
                for c in range(CHUNKS):
                    for p in pieces_of(t, c):
                        act.wait_ge(stage_loaded[p % STAGES], 16 * (p // STAGES + 1))
                        act.copy(piece(p, True), stage[:, p % STAGES, :]).then_inc(w_hi_ready, 1)
                    if c + 1 < CHUNKS:
                        split_high(t, c + 1)
                    elif not is_number(t, TILES - 1):
                        split_high(t + 1, 0)
                    if not is_number(t, 0):
                        chain(t - 1, c)

            split_high(0, 0)
            over_tiles(act, tile)
            for c in range(CHUNKS):
                chain(TILES - 1, c)

        @block.vector
        def _(dve):
            dve.memset(up[G:P, :, :], 0.0).then_inc(zeroed, 1)
            dve.memset(hidden[G:P, :], 0.0).then_inc(zeroed, 1)
            dve.memset(hidden[0:G, :], 0.0).then_inc(zeroed, 1)
            dve.wait_ge(zeroed, 3)
            dve.memset(hidden[G:G + 1, :], 1.0).then_inc(zeroed, 1)
            dve.wait_ge(consts_loaded, 32)
            dve.tensor_scalar(row[:, :, :], adapter[:, :, :], float(RANK), rank_row[:, 0:1], ALU.mult, ALU.add)\
               .then_inc(row_ready, 1)
            dve.wait_ge(own_ready, 16)

            def split_low(t, c):
                n, par = CHUNKS * t + c, c % 2
                dve.wait_ge(o_hi_ready, n + 1)
                dve.tensor_tensor(ol[:, par, :, :].rearrange("d h (b s) -> d h b s", b=BPT),
                                  o_raw[:, par, :, :, :].rearrange("d b h s -> d h b s"),
                                  oh[:, par, :, :].bitcast(F32).rearrange("d h (b s) -> d h b s", b=BPT),
                                  ALU.subtract).then_inc(o_lo_ready, 1)

            def chain(t, c):
                if c in TURN_SLOT and TURN_SLOT[c] in HAS_BASE:
                    k = 3 * t + TURN_SLOT[c]
                    dve.wait_ge(xTh_ready, 2 * t + HAS_BASE[TURN_SLOT[c]] + 1)
                    dve.wait_ge(xT_ready, k + 1)
                    dve.tensor_tensor(xTl[:, :, :], ps[:, 2, :].rearrange("i (k r) -> i k r", k=KT),
                                      xTh[:, :, :].bitcast(F32), ALU.subtract).then_inc(xTl_ready, 1)
                if c in HIDDEN_SLOT:
                    layer = HIDDEN_SLOT[c]
                    k = 3 * t + layer
                    dve.wait_ge(hidden_done, k + 1)
                    wait(dve, layer_done, k)
                    dve.scalar_tensor_tensor(out=hidden[0:G, :], in0=ps[0:G, 4, 0:P],
                                             scalar=LORA_SCALE if layer == 2 else 1.0, in1=own[:, :],
                                             op0=ALU.mult, op1=ALU.mult).then_inc(hidden_ready, 1)
                if c in END_SLOT:
                    layer = END_SLOT[c]
                    k = 3 * t + layer
                    if layer == 0:
                        wait(dve, out_stored, 16 * t)
                        dve.wait_ge(x1_ready, t + 1)
                    else:
                        dve.wait_ge(x_ready, k)
                    dve.wait_ge(layer_done, k + 1)
                    dve.tensor_tensor(x_now[:, (layer + 1) % 2, :], x_now[:, layer % 2, :], ps[:, 5 + layer, :],
                                      ALU.add).then_inc(x_ready, 1)

            def tile(t, par):
                for c in range(CHUNKS):
                    for p in pieces_of(t, c):
                        dve.wait_ge(w_hi_ready, p + 1)
                        dve.tensor_tensor(piece(p, False), stage[:, p % STAGES, :],
                                          piece(p, True).bitcast(F32), ALU.subtract).then_inc(w_lo_ready, 1)
                    if c + 1 < CHUNKS:
                        split_low(t, c + 1)
                    elif not is_number(t, TILES - 1):
                        split_low(t + 1, 0)
                    if not is_number(t, 0):
                        chain(t - 1, c)
                dve.wait_ge(x_loaded, 16 * (t + 1))
                dve.wait_ge(o_used, CHUNKS * (t + 1))
                wait(dve, x_ready, 3 * t)
                dve.tensor_tensor(x_now[:, 0, :], x_in[:, :], ps[:, par, :], ALU.add).then_inc(x1_ready, 1)

            split_low(0, 0)
            over_tiles(dve, tile)
            for c in range(CHUNKS):
                chain(TILES - 1, c)

        @block.tensor
        def _(pe):
            pe.wait_ge(ident_ready, 2)
            pe.wait_ge(zeroed, 4)

            def project_chunk(t, par, c):
                pe.wait_ge(o_lo_ready, CHUNKS * t + c + 1)
                if c == 0:
                    wait(pe, x1_ready, t - 1)
                for h in range(QUARTER):
                    if is_number(t, 0):
                        pe.wait_ge(w_lo_ready, QUARTER * c + h + 1)
                    for o_part, w_part in ((oh, woh), (ol, woh), (oh, wol)):
                        last = pe.matmul(ps[:, par, :], o_part[:, c % 2, h, :], w_part[:, QUARTER * c + h, :],
                                         start=(c == 0 and h == 0 and o_part is oh and w_part is woh),
                                         stop=(c == CHUNKS - 1 and h == QUARTER - 1 and w_part is wol))
                last.then_inc(o_used, 1)

            def chain(t, c):
                if c in TURN_SLOT:
                    layer = TURN_SLOT[c]
                    k = 3 * t + layer
                    if layer == 0:
                        pe.wait_ge(x1_ready, t + 1)
                    else:
                        pe.wait_ge(x_ready, k)
                    wait(pe, xT_ready, k)
                    wait(pe, xTl_ready, 2 * t + (layer + 1) // 2)
                    for kt in range(KT):
                        last = pe.transpose(ps[:, 2, P * kt:P * kt + P],
                                            x_now[:, layer % 2, P * kt:P * kt + P], ident[:, :])
                    last.then_inc(x_turned, 1)
                    wait_all(pe, pe_passed, (adapters_loaded[layer], 32 * (t + 1)), (downT_ready, k))
                    for kt in range(KT):
                        last = pe.transpose(ps[:, 3, G * kt:G * kt + G], down[:, layer, P * kt:P * kt + P],
                                            ident[0:G, 0:G])
                    last.then_inc(down_turned, 1)
                if c in HIDDEN_SLOT:
                    layer = HIDDEN_SLOT[c]
                    k = 3 * t + layer
                    pe.wait_ge(xT_ready, k + 1)
                    pe.wait_ge(downT_ready, k + 1)
                    wait(pe, hidden_ready, k)
                    for kt in range(KT):
                        last = pe.matmul(ps[0:G, 4, 0:P], downT[:, kt, :], xT[:, kt, :],
                                         start=(kt == 0), stop=(kt == KT - 1))
                    last.then_inc(hidden_done, 1)
                    if layer in HAS_BASE:
                        base = HAS_BASE[layer]
                        wait(pe, x_ready, k - 2)
                        pe.wait_ge(xTl_ready, 2 * t + base + 1)
                        for kt in range(KT):
                            for x_part, w_part in ((xTh, bwh), (xTl, bwh), (xTh, bwl)):
                                pe.matmul(ps[:, 5 + layer, :], x_part[:, kt, :], w_part[:, base, kt, :],
                                          start=(kt == 0 and x_part is xTh and w_part is bwh), stop=False)
                if c in END_SLOT:
                    layer = END_SLOT[c]
                    k = 3 * t + layer
                    pe.wait_ge(hidden_ready, k + 1)
                    pe.matmul(ps[:, 5 + layer, :], hidden[:, :], up[:, layer, :],
                              start=(layer not in HAS_BASE), stop=True).then_inc(layer_done, 1)

            def tile(t, par):
                for c in range(CHUNKS):
                    project_chunk(t, par, c)
                    if is_number(t, 1) and c == 0:
                        pe.wait_ge(w_lo_ready, PIECES)
                        pe.wait_ge(bias_loaded, 32)
                    if not is_number(t, 0):
                        chain(t - 1, c)

            over_tiles(pe, tile)
            for c in range(CHUNKS):
                chain(TILES - 1, c)


def build(nc, a, out):
    scratch = {
        "k": nc.dram_tensor("k_scratch", (BATCH, D, HK, SEQ), F32, kind="Internal").ap(),
        "v": nc.dram_tensor("v_scratch", (TOKENS, HK * D), F32, kind="Internal").ap(),
        "q": nc.dram_tensor("q_scratch", (BATCH, D, HQ, SEQ), F32, kind="Internal").ap(),
        "o": nc.dram_tensor("o_scratch", (BATCH, D, HQ, SEQ), F32, kind="Internal").ap(),
    }
    with nc.psum_tensor("banks", [P, 8, 512], F32) as ps:
        project(nc, ps, a, scratch)
        attend(nc, ps, a, scratch)
        finish(nc, ps, a, scratch, out)


def lay_out(x, itok_Bx16_0_63, itok_B_207_1644, itok_B_6_15, itok_B_3_7, itok_B_0_23, L0_cond_Wq, L0_cond_Wk,
            L0_cond_Wv, L0_cond_Wo, L0_cond_q_norm_w, L0_cond_k_norm_w, L0_cond_k_cache, L0_cond_v_cache,
            L1_cond_base_weight, L1_cond_base_bias, L1_cond_lora_A_w, L1_cond_lora_B_w, L2_cond_A, L2_cond_B,
            L3_cond_W, L3_cond_b, L3_cond_lora_As, L3_cond_lora_Bs):
    def by_k(w):
        return w.T.reshape(KT, P, -1).transpose(1, 0, 2)

    wq = L0_cond_Wq.reshape(HK, REP, D, HID).transpose(1, 0, 2, 3).reshape(HQ * D, HID)
    w_all = np.concatenate([L0_cond_Wv, L0_cond_Wk, wq, L0_cond_Wv[:CH]])
    tile_of = np.arange(P) // SEQ
    flat_x = x.reshape(TOKENS, HID)
    seqlen = itok_B_207_1644
    adapters = np.stack([itok_B_6_15, itok_B_3_7, itok_B_0_23])
    return {
        "x": flat_x,
        "xT": flat_x.T.reshape(KT, P, X_PIECES, X_COLS).transpose(1, 2, 0, 3),
        "w_all": w_all.reshape(-1, CH, KT, P).transpose(0, 3, 2, 1),
        "seqlen_by_tile": seqlen.reshape(TILES, BPT).T[tile_of],
        "seqlen_all": np.broadcast_to(seqlen, (P, BATCH)),
        "row_in_seq": (np.arange(P) % SEQ).astype(np.float32).reshape(P, 1),
        "inv_freq": np.broadcast_to(
            (np.float32(1) / np.float32(THETA) ** (np.arange(0, D, 2, dtype=np.float32) / np.float32(D)))
            .astype(np.float32), (P, D // 2)),
        "k_norm": np.broadcast_to(L0_cond_k_norm_w, (P, D)),
        "q_norm": np.broadcast_to(L0_cond_q_norm_w, (P, D)),
        "k_cacheT": L0_cond_k_cache.transpose(3, 0, 2, 1),
        "v_rows": L0_cond_v_cache.reshape(PAGES * PSIZE, HK * D),
        "block_table": itok_Bx16_0_63,
        "page_of_row": itok_Bx16_0_63.reshape(BATCH, CACHED // P, BPT)[:, :, tile_of].transpose(2, 0, 1)
        .reshape(P, BATCH * CACHED // P),
        "row_in_page": (np.arange(P) % PSIZE).astype(np.float32).reshape(P, 1),
        "woT": L0_cond_Wo.T.reshape(HQ, D, HID).transpose(1, 0, 2),
        "baseT": np.stack([by_k(L1_cond_base_weight), by_k(L3_cond_W)], axis=1),
        "bias1": L1_cond_base_bias.reshape(1, HID),
        "bias3": L3_cond_b.reshape(1, HID),
        "down1": L1_cond_lora_A_w.reshape(-1, HID),
        "up1": L1_cond_lora_B_w.transpose(0, 2, 1).reshape(-1, HID),
        "down2": L2_cond_B.reshape(-1, HID),
        "up2": L2_cond_A.transpose(0, 2, 1).reshape(-1, HID),
        "down3": L3_cond_lora_As.transpose(0, 2, 1).reshape(-1, HID),
        "up3": L3_cond_lora_Bs.reshape(-1, HID),
        "adapter_by_tile": adapters.reshape(3, TILES, BPT)[:, :, np.arange(BPT * RANK) // RANK].transpose(2, 0, 1),
        "rank_row": (np.arange(BPT * RANK) % RANK).astype(np.float32).reshape(-1, 1),
        "own": (np.arange(BPT * RANK)[:, None] // RANK == np.arange(P)[None, :] // SEQ).astype(np.float32),
    }


def kernel(**inputs):
    import concourse.bacc as bacc
    from concourse.bass_utils import run_bass_kernel_spmd

    nc = bacc.Bacc("TRN2", target_bir_lowering=False, num_devices=1)
    arrays, aps = {}, {}
    for name, value in lay_out(**{k: np.asarray(v) for k, v in inputs.items()}).items():
        arrays[f"in_{name}"] = value = np.ascontiguousarray(value)
        aps[name] = nc.dram_tensor(f"in_{name}", value.shape, mybir.dt.from_np(value.dtype),
                                   kind="ExternalInput").ap()
    out = nc.dram_tensor("out_x", (TOKENS, HID), F32, kind="ExternalOutput").ap()
    build(nc, aps, out)
    result = run_bass_kernel_spmd(nc, [arrays], core_ids=[0])
    return result.results[0]["out_x"].reshape(BATCH, SEQ, HID)
```
